# Optimizing a Trainium2 kernel written in Bass

```python
import numpy as np
import jax
import jax.numpy as jnp

def _softmax(x, axis=-1):
    return jax.nn.softmax(x, axis=axis)

def _gelu(x):
    return jax.nn.gelu(x, approximate=True)

def _silu(x):
    return jax.nn.silu(x)

def _sigmoid(x):
    return jax.nn.sigmoid(x)

def _layernorm(x, axis=-1, eps=1e-05):
    m = jnp.mean(x, axis=axis, keepdims=True)
    v = jnp.var(x, axis=axis, keepdims=True)
    return (x - m) / jnp.sqrt(v + eps)

def _scatter_add(tgt, idx, src, axis=0):
    return tgt.at[idx].add(src)

def _segment_sum(src, seg, n):
    return jax.ops.segment_sum(src, seg, n)
kernel_name = 'mk_recurrent_d1_jaxref_r8_5989d0'

def setup_inputs(seed: int=0):
    np.random.seed(seed)
    _w = jnp.asarray

    def _L0_attn_setup():
        import jax, jax.numpy as jnp
        import numpy as np
        import math
        B, S, DM = (1, 256, 512)
        H, HKV, HD = (32, 8, 128)
        EPS = 1e-06
        NEG_INF = -1e+30

        def _alibi_slopes(n_heads: int) -> np.ndarray:
            start = 2 ** (-2 ** (-(math.log2(n_heads) - 3)))
            return np.array([start * start ** i for i in range(n_heads)], dtype=np.float32)

        def _rmsnorm(t, w):
            tf = t.astype(jnp.float32)
            inv = jax.lax.rsqrt(jnp.mean(tf * tf, axis=-1, keepdims=True) + EPS)
            return (tf * inv * w).astype(t.dtype)
        key = jax.random.key(seed)
        ks = jax.random.split(key, 5)
        std = 0.02
        return {'x': jax.random.normal(ks[0], (B, S, DM), dtype=jnp.float32), 'Wq': jax.random.normal(ks[1], (H * HD, DM), dtype=jnp.float32) * std, 'Wk': jax.random.normal(ks[2], (HKV * HD, DM), dtype=jnp.float32) * std, 'Wv': jax.random.normal(ks[3], (HKV * HD, DM), dtype=jnp.float32) * std, 'Wo': jax.random.normal(ks[4], (H * HD, DM), dtype=jnp.float32).T * (std / math.sqrt(2 * 32)), 'q_norm_w': jnp.ones((HD,), dtype=jnp.float32), 'k_norm_w': jnp.ones((HD,), dtype=jnp.float32)}
    _L0_attn_in = _L0_attn_setup()

    def _L0_ffn_setup():
        import jax, jax.numpy as jnp
        import numpy as np
        ALPHA = 32
        R = 16
        SCALING = ALPHA / R
        key = jax.random.key(seed)
        k1, k2, k3, k4 = jax.random.split(key, 4)
        B_, S, D = (4, 256, 512)
        H, r, O = (8, R, 512)
        x = jax.random.normal(k1, (B_, S, D), dtype=jnp.float32)
        A = jax.random.normal(k2, (H, r, D), dtype=jnp.float32) * 0.02
        Bm = jax.random.normal(k3, (H, O, r), dtype=jnp.float32) * 0.02
        Wr = jax.random.normal(k4, (H, D), dtype=jnp.float32) * 0.02
        br = jnp.zeros((H,), dtype=jnp.float32)
        return {'x': x, 'A': A, 'B': Bm, 'Wr': Wr, 'br': br}
    _L0_ffn_in = _L0_ffn_setup()
    _d = {'L0_attn_x': _L0_attn_in['x'], 'L0_attn_Wq': _L0_attn_in['Wq'], 'L0_attn_Wk': _L0_attn_in['Wk'], 'L0_attn_Wv': _L0_attn_in['Wv'], 'L0_attn_Wo': _L0_attn_in['Wo'], 'L0_attn_q_norm_w': _L0_attn_in['q_norm_w'], 'L0_attn_k_norm_w': _L0_attn_in['k_norm_w'], 'L0_ffn_A': _L0_ffn_in['A'], 'L0_ffn_B': _L0_ffn_in['B'], 'L0_ffn_Wr': _L0_ffn_in['Wr'], 'L0_ffn_br': _L0_ffn_in['br']}
    _x0 = _d['L0_attn_x']
    _d['L0_attn_x'] = jax.random.normal(jax.random.fold_in(jax.random.key(seed), 1), (2, 512, 512), dtype=_x0.dtype)
    del _x0
    return _d

def reference(L0_attn_x, L0_attn_Wq, L0_attn_Wk, L0_attn_Wv, L0_attn_Wo, L0_attn_q_norm_w, L0_attn_k_norm_w, L0_ffn_A, L0_ffn_B, L0_ffn_Wr, L0_ffn_br):

    def _L0_attn_ref(x, Wq, Wk, Wv, Wo, q_norm_w, k_norm_w):
        import jax, jax.numpy as jnp
        import numpy as np
        import math
        B, S, DM = (1, 256, 512)
        H, HKV, HD = (32, 8, 128)
        EPS = 1e-06
        NEG_INF = -1e+30

        def _alibi_slopes(n_heads: int) -> np.ndarray:
            start = 2 ** (-2 ** (-(math.log2(n_heads) - 3)))
            return np.array([start * start ** i for i in range(n_heads)], dtype=np.float32)

        def _rmsnorm(t, w):
            tf = t.astype(jnp.float32)
            inv = jax.lax.rsqrt(jnp.mean(tf * tf, axis=-1, keepdims=True) + EPS)
            return (tf * inv * w).astype(t.dtype)
        b, s, _ = x.shape
        G = H // HKV
        q = (x @ Wq.T).reshape(b, s, H, HD).transpose(0, 2, 1, 3)
        k = (x @ Wk.T).reshape(b, s, HKV, HD).transpose(0, 2, 1, 3)
        v = (x @ Wv.T).reshape(b, s, HKV, HD).transpose(0, 2, 1, 3)
        q = _rmsnorm(q, q_norm_w)
        k = _rmsnorm(k, k_norm_w)
        qg = q.reshape(b, HKV, G, s, HD)
        scores = jnp.einsum('bkgqd,bksd->bkgqs', qg, k) / math.sqrt(HD)
        slopes = jnp.asarray(_alibi_slopes(H)).reshape(HKV, G)
        pos = jnp.arange(s, dtype=jnp.float32)
        rel = pos[None, :] - pos[:, None]
        bias = jnp.where(rel > 0, NEG_INF, slopes[:, :, None, None] * rel)
        attn = jax.nn.softmax(scores + bias[None], axis=-1)
        out = jnp.einsum('bkgqs,bksd->bkgqd', attn, v)
        out = out.reshape(b, H, s, HD).transpose(0, 2, 1, 3).reshape(b, s, H * HD)
        return out @ Wo.T

    def _L0_ffn_ref(x, A, B, Wr, br):
        import jax, jax.numpy as jnp
        import numpy as np
        ALPHA = 32
        R = 16
        SCALING = ALPHA / R
        H = A.shape[0]
        router_logits = jnp.einsum('bsd,hd->bsh', x, Wr) + br
        scores = H * jax.nn.softmax(router_logits, axis=-1)
        low = jnp.einsum('bsd,hrd->bshr', x, A)
        out = jnp.einsum('bshr,hor,bsh->bso', low, B, scores)
        return SCALING * out
    x = L0_attn_x
    xn = _layernorm(x, axis=-1)
    s = _L0_attn_ref(xn, L0_attn_Wq, L0_attn_Wk, L0_attn_Wv, L0_attn_Wo, L0_attn_q_norm_w, L0_attn_k_norm_w)
    g = _silu(_L0_ffn_ref(xn, L0_ffn_A, L0_ffn_B, L0_ffn_Wr, L0_ffn_br))
    x = x + s * g
    return x

_drawn_inputs = setup_inputs


def setup_inputs(seed=0):
    import zlib

    import numpy as np

    out = dict(_drawn_inputs(seed))
    spreads = {'L0_attn_q_norm_w': (1.0, 0.6), 'L0_attn_k_norm_w': (1.0, 0.6), 'L0_ffn_br': (0.0, 0.8)}
    factors = {'L0_attn_Wq': 8.0,
     'L0_attn_Wk': 8.0,
     'L0_attn_Wv': 8.0,
     'L0_attn_Wo': 8.0,
     'L0_ffn_A': 8.0,
     'L0_ffn_B': 8.0,
     'L0_ffn_Wr': 8.0}
    for name, (base, spread) in spreads.items():
        noise = np.random.default_rng([zlib.crc32(name.encode()), seed]).standard_normal(out[name].shape)
        drawn = base * np.exp(spread * noise) if base else spread * noise
        out[name] = jnp.asarray(drawn.astype(out[name].dtype))
    for name, factor in factors.items():
        out[name] = (out[name] * factor).astype(out[name].dtype)
    return out
```

```python
from contextlib import ExitStack

import numpy as np

import concourse.bass as bass
from concourse import mybir

F32 = mybir.dt.float32
F32R = mybir.dt.float32r
ALU = mybir.AluOpType
ACT = mybir.ActivationFunctionType
AX = mybir.AxisListType

P = 128
BATCH, SEQ, DM = 2, 512, 512
HEADS, GROUPS, HD = 32, 8, 128
HPG = HEADS // GROUPS
QB = SEQ // P
BLOCKS = BATCH * QB
UNITS = GROUPS * BLOCKS
KC = DM // P
QW = HPG * HD
NORMED = HPG + 1
QK = NORMED * HD
QKV = QK + HD
EXPERTS, RANK = 8, 16
LOW = EXPERTS * RANK
AW = 256
FFN_SCALE = 2.0 * EXPERTS
LN_EPS, RMS_EPS = 1e-5, 1e-6
MASKED = 1e30
HUGE = 3e38
EXP_FLOOR = -87.0

C_IDENT = 0
C_DIST = C_IDENT + P
C_SLOPE = C_DIST + SEQ
C_FACTOR = C_SLOPE + HEADS
C_END = C_FACTOR + GROUPS * NORMED


def constants():
    import math
    start = 2 ** (-2 ** (-(math.log2(HEADS) - 3)))
    slopes = np.array([start * start ** i for i in range(HEADS)], dtype=np.float32)
    c = np.zeros((P, C_END), np.float32)
    c[:, C_IDENT:C_DIST] = np.eye(P)
    d = np.arange(P)[:, None] + (SEQ - P) - np.arange(SEQ)[None, :]
    c[:, C_DIST:C_SLOPE] = np.where(d < 0, MASKED, d)
    c[:, C_SLOPE:C_FACTOR] = slopes
    f = np.ones((GROUPS, NORMED))
    f[:, :HPG] = -1.0 / (slopes.astype(np.float64).reshape(GROUPS, HPG) * math.sqrt(HD))
    c[:, C_FACTOR:] = f.reshape(1, -1)
    return c


def counter(per_unit):
    n = len(per_unit)

    def value(g, t, e):
        return g * sum(per_unit) + (t // n) * sum(per_unit) + sum(per_unit[:t % n]) + e
    return value


ONE = counter([1] * BLOCKS)
TWO = counter([2] * BLOCKS)
PER_HEAD = counter([HPG] * BLOCKS)
PER_KEY_BLOCK = counter([i + 1 for i in range(QB)] * BATCH)
QK_PARTS = counter(([1] + [2] * (QB - 1)) * BATCH)


def keys_of(t):
    return t % QB + 1


def build(nc, x, wqkv, wo, aw, bt, br, qkw, consts, y):
    with ExitStack() as ctx:
        def sb(name, shape, dt=F32):
            return ctx.enter_context(nc.sbuf_tensor(name, [P, *shape], dt))

        def psum(name, shape):
            return ctx.enter_context(nc.psum_tensor(name, [P, *shape], F32))

        def sem(name):
            return ctx.enter_context(nc.semaphore(name))

        cst = sb("cst", [C_END])
        ident = cst[:, C_IDENT:C_DIST]
        qkw_sb = sb("qkw_sb", [2])
        br_sb = sb("br_sb", [EXPERTS])
        x_sb = sb("x_sb", [BLOCKS, DM])
        xt_hi, xt_lo = (sb(f"xt_{p}", [KC, BLOCKS * P], F32R) for p in ("hi", "lo"))
        w_raw = sb("w_raw", [KC, QKV])
        w_hi, w_lo = (sb(f"w_{p}", [KC, QKV], F32R) for p in ("hi", "lo"))
        wo_raw = sb("wo_raw", [HPG, DM])
        wo_hi, wo_lo = (sb(f"wo_{p}", [HPG, DM], F32R) for p in ("hi", "lo"))
        bt_hi, bt_lo = (sb(f"bt_{p}", [DM], F32R) for p in ("hi", "lo"))
        squares = sb("squares", [NORMED, HD])
        qk_norm = sb("qk_norm", [NORMED, HD])
        q_full = sb("q_full", [QW])
        k_full = sb("k_full", [P])
        q_hi, q_lo = (sb(f"q_{p}", [QW], F32R) for p in ("hi", "lo"))
        k_hi, k_lo = (sb(f"k_{p}", [BATCH, SEQ], F32R) for p in ("hi", "lo"))
        v_hi, v_lo = (sb(f"v_{p}", [BATCH, QB, HD], F32R) for p in ("hi", "lo"))
        probs = sb("probs", [HPG, SEQ])
        pt_hi, pt_lo = (sb(f"pt_{p}", [QB, HPG * P], F32R) for p in ("hi", "lo"))
        o_hi, o_lo = (sb(f"o_{p}", [HPG * P], F32R) for p in ("hi", "lo"))
        acc = sb("acc", [BLOCKS, DM])
        gate = sb("gate", [BLOCKS, DM])
        slope = sb("slope", [HPG])
        factor = sb("factor", [NORMED])
        sums = sb("sums", [NORMED])
        mean_sq = sb("mean_sq", [NORMED])
        inv_rms = sb("inv_rms", [NORMED])
        inv = sb("inv", [NORMED])
        minus_half = sb("minus_half", [8])
        neg_max = sb("neg_max", [HPG])
        total = sb("total", [HPG])
        recip = sb("recip", [HPG])
        bn = sb("bn", [BLOCKS, 6])
        moments = sb("moments", [BLOCKS, 2])
        var_eps = sb("var_eps", [BLOCKS])
        rstd = sb("rstd", [BLOCKS])
        logits = sb("logits", [2, EXPERTS])
        logit_max = sb("logit_max", [2])
        route = sb("route", [2, EXPERTS])
        route_sum = sb("route_sum", [2])
        route_inv = sb("route_inv", [2])
        low = probs[:, 0, 0:2 * LOW].rearrange("p (s l) -> p s l", s=2)
        sig = probs[:, 1:3, :]
        aw_raw = sb("aw_raw", [KC, LOW + EXPERTS])
        aw_hi = pt_hi[:, 0:2, :].rearrange("p a (b n) -> p (a b) n", b=2)
        aw_lo = pt_lo[:, 0:2, :].rearrange("p a (b n) -> p (a b) n", b=2)
        lt_hi = pt_hi[:, 2, 0:2 * P].rearrange("p (s n) -> p s n", s=2)
        lt_lo = pt_lo[:, 2, 0:2 * P].rearrange("p (s n) -> p s n", s=2)
        bt_raw = squares[:, 0:HPG, :].rearrange("p a n -> p (a n)")

        qkv_ps = psum("qkv_ps", [2, 512])
        score_ps = psum("score_ps", [2, 512])
        turn_ps = psum("turn_ps", [2, 512])
        mix_ps = psum("mix_ps", [512])
        out_ps = psum("out_ps", [512])
        qkv_flat = qkv_ps[:, :, :].rearrange("p a n -> p (a n)")
        v_ps = qkv_flat[:, QK:QKV]
        gate_ps = [mix_ps, out_ps]

        x_loaded = [sem(f"x_loaded{t}") for t in range(BLOCKS)]
        small_loaded = sem("small_loaded")
        ffn_loaded = sem("ffn_loaded")
        w_loaded = sem("w_loaded")
        wo_loaded = sem("wo_loaded")
        x_again = sem("x_again")
        stored = sem("stored")
        half_set = sem("half_set")
        bn_done = sem("bn_done")
        moments_done = sem("moments_done")
        var_done = sem("var_done")
        rstd_done = sem("rstd_done")
        xn_done = sem("xn_done")
        xt_turned = sem("xt_turned")
        xt_hi_done = sem("xt_hi_done")
        xt_lo_done = sem("xt_lo_done")
        aw_zeroed = sem("aw_zeroed")
        ffn_hi_done = sem("ffn_hi_done")
        ffn_lo_done = sem("ffn_lo_done")
        low_done = sem("low_done")
        logits_done = sem("logits_done")
        logit_max_done = sem("logit_max_done")
        route_done = sem("route_done")
        route_inv_done = sem("route_inv_done")
        route_scaled = sem("route_scaled")
        low_scaled = sem("low_scaled")
        low_turned = sem("low_turned")
        lt_hi_done = sem("lt_hi_done")
        lt_lo_done = sem("lt_lo_done")
        gate_in_done = sem("gate_in_done")
        gate_in_capped = sem("gate_in_capped")
        gate_exp_done = sem("gate_exp_done")
        gate_plus_done = sem("gate_plus_done")
        gate_recip_done = sem("gate_recip_done")
        gate_done = sem("gate_done")
        w_hi_done = sem("w_hi_done")
        w_lo_done = sem("w_lo_done")
        wo_hi_done = sem("wo_hi_done")
        wo_lo_done = sem("wo_lo_done")
        slope_set = sem("slope_set")
        factor_set = sem("factor_set")
        qkv_ready = sem("qkv_ready")
        squares_ready = sem("squares_ready")
        sums_ready = sem("sums_ready")
        mean_sq_ready = sem("mean_sq_ready")
        inv_rms_ready = sem("inv_rms_ready")
        inv_ready = sem("inv_ready")
        qk_norm_ready = sem("qk_norm_ready")
        v_hi_ready = sem("v_hi_ready")
        v_lo_ready = sem("v_lo_ready")
        qk_turned = sem("qk_turned")
        qk_hi_ready = sem("qk_hi_ready")
        qk_lo_ready = sem("qk_lo_ready")
        scores_ready = sem("scores_ready")
        scores_taken = sem("scores_taken")
        biased_ready = sem("biased_ready")
        exp_ready = sem("exp_ready")
        recip_ready = sem("recip_ready")
        probs_ready = sem("probs_ready")
        probs_turned = sem("probs_turned")
        pt_hi_ready = sem("pt_hi_ready")
        pt_lo_ready = sem("pt_lo_ready")
        mix_ready = sem("mix_ready")
        o_hi_ready = sem("o_hi_ready")
        o_lo_ready = sem("o_lo_ready")
        out_ready = sem("out_ready")
        acc_ready = sem("acc_ready")
        gated_ready = sem("gated_ready")
        y_ready = sem("y_ready")

        def turn_slot(s, n):
            per = [keys_of(i) + 2 for i in range(QB)]
            return (sum(per) * (s // QB) + sum(per[:s % QB]) + n) % 2

        def pipeline(eng, slot):
            for t in (-2, -1, 0):
                slot(0, t, GROUPS)
            with eng.Fori(0, GROUPS - 1) as g:
                for t in range(1, BLOCKS + 1):
                    slot(g, t, GROUPS)
            for t in range(1, BLOCKS + 1):
                slot(GROUPS - 1, t, 1)

        def here(t, left):
            return 0 <= t < BLOCKS * left

        block = ctx.enter_context(nc.Block())

        @block.sync
        def _(sp):
            for t in range(BLOCKS):
                sp.dma_start(x_sb[:, t, :], x[t * P:(t + 1) * P, :]).then_inc(x_loaded[t], 16)
            sp.dma_start(aw_raw[:, :, :].rearrange("p c n -> p (c n)"), aw).then_inc(ffn_loaded, 16)
            sp.dma_start(bt_raw, bt).then_inc(ffn_loaded, 16)
            sp.dma_start(wo_raw[:, :, :].rearrange("p c n -> p (c n)"), wo[0:1].rearrange("a p n -> p (a n)")).then_inc(wo_loaded, 16)
            sp.wait_ge(xt_turned, BLOCKS)
            sp.dma_start(x_sb[:, :, :], x.rearrange("(t p) n -> p t n", p=P)).then_inc(x_again, 16)
            with sp.Fori(0, GROUPS - 1) as g:
                sp.wait_ge(w_lo_done, g * KC + KC)
                sp.dma_start(w_raw[:, :, :].rearrange("p c n -> p (c n)"), wqkv[bass.ds(g + 1, 1)].rearrange("a p n -> p (a n)")).then_inc(w_loaded, 16)
                sp.wait_ge(wo_lo_done, g * HPG + HPG)
                sp.dma_start(wo_raw[:, :, :].rearrange("p c n -> p (c n)"), wo[bass.ds(g + 1, 1)].rearrange("a p n -> p (a n)")).then_inc(wo_loaded, 16)
            for t in range(BLOCKS):
                sp.wait_ge(y_ready, t + 1)
                sp.dma_start(y[t * P:(t + 1) * P, :], acc[:, t, :]).then_inc(stored, 16)
            sp.wait_ge(stored, 16 * BLOCKS)

        @block.gpsimd
        def _(pool):
            nc.gpsimd.memset(minus_half[:, :], -0.5).then_inc(half_set, 1)
            nc.gpsimd.memset(acc[:, :, :], 0.0).then_inc(acc_ready, 1)
            pool.wait_ge(half_set, 1)
            pool.wait_ge(var_done, 1)
            nc.gpsimd.tensor_tensor(rstd[:, :], var_eps[:, :], minus_half[:, 0:BLOCKS], ALU.pow).then_inc(rstd_done, 1)

            def slot(g, t, left):
                if here(t + 2, left):
                    pool.wait_ge(mean_sq_ready, ONE(g, t + 2, 1))
                    nc.gpsimd.tensor_tensor(inv_rms[:, :], mean_sq[:, :], minus_half[:, 0:NORMED],
                                            ALU.pow).then_inc(inv_rms_ready, 1)
            pipeline(pool, slot)

        @block.scalar
        def _(act):
            act.dma_start(cst[:, :], consts).then_inc(small_loaded, 16)
            act.dma_start(qkw_sb[:, :], qkw).then_inc(small_loaded, 16)
            act.dma_start(br_sb[:, :], br).then_inc(small_loaded, 16)
            act.dma_start(w_raw[:, :, :].rearrange("p c n -> p (c n)"), wqkv[0:1].rearrange("a p n -> p (a n)")).then_inc(w_loaded, 16)

            def split_w(g, group):
                act.wait_ge(w_loaded, group * 16 + 16)
                for c in range(KC):
                    nc.scalar.activation(w_hi[:, c, :], w_raw[:, c, :], ACT.Copy).then_inc(w_hi_done, 1)

            def split_wo(group):
                act.wait_ge(wo_loaded, group * 16 + 16)
                for h in range(HPG):
                    nc.scalar.activation(wo_hi[:, h, :], wo_raw[:, h, :], ACT.Copy).then_inc(wo_hi_done, 1)

            for t in range(BLOCKS):
                act.wait_ge(xt_turned, t + 1)
                nc.scalar.activation(xt_hi[:, :, t * P:(t + 1) * P],
                                     turn_ps[:, t % 2, :].rearrange("p (c n) -> p c n", c=KC),
                                     ACT.Copy).then_inc(xt_hi_done, 1)
            act.wait_ge(ffn_loaded, 32)
            act.wait_ge(aw_zeroed, 1)
            for c in range(KC):
                nc.scalar.activation(aw_hi[:, c, 0:LOW + EXPERTS], aw_raw[:, c, :], ACT.Copy).then_inc(ffn_hi_done, 1)
            nc.scalar.activation(bt_hi[:, :], bt_raw, ACT.Copy).then_inc(ffn_hi_done, 1)
            split_w(0, 0)
            for t in range(BLOCKS):
                if True:
                    act.wait_ge(logit_max_done, t + 1)
                    nc.scalar.activation(route[:, t % 2, :], logits[:, t % 2, :], ACT.Exp, bias=logit_max[:, t % 2:t % 2 + 1],
                                         accum_out=route_sum[:, t % 2:t % 2 + 1]).then_inc(route_done, 1)
                    act.wait_ge(low_turned, t + 1)
                    nc.scalar.activation(lt_hi[:, t % 2, :], turn_ps[:, t % 2, 0:P], ACT.Copy).then_inc(lt_hi_done, 1)
                    act.wait_ge(gate_in_capped, t + 1)
                    nc.scalar.activation(sig[:, t % 2, :], sig[:, t % 2, :], ACT.Exp, scale=-1.0).then_inc(gate_exp_done, 1)

            def slot(g, t, left):
                i = t % QB
                n = keys_of(t) * P
                if here(t, left):
                    for h in range(HPG):
                        act.wait_ge(biased_ready, PER_HEAD(g, t, h + 1))
                        nc.scalar.activation(probs[:, h, 0:n], probs[:, h, 0:n], ACT.Exp, bias=neg_max[:, h:h + 1],
                                             scale=-1.0, accum_out=total[:, h:h + 1]).then_inc(exp_ready, 1)
                if here(t + 1, left):
                    u, b, ui = t + 1, (t + 1) // QB % BATCH, (t + 1) % QB
                    if ui > 0:
                        act.wait_ge(qk_turned, TWO(g, u, 1))
                        nc.scalar.activation(q_hi[:, :], turn_ps[:, turn_slot(t, 0), :], ACT.Copy,
                                             scale=qkw_sb[:, 0:1]).then_inc(qk_hi_ready, 1)
                    act.wait_ge(qk_turned, TWO(g, u, 2))
                    nc.scalar.activation(k_hi[:, b, ui * P:(ui + 1) * P], turn_ps[:, turn_slot(t, 1), 0:P], ACT.Copy,
                                         scale=qkw_sb[:, 1:2]).then_inc(qk_hi_ready, 1)

                def turned_hi(j):
                    act.wait_ge(probs_turned, PER_KEY_BLOCK(g, t, j + 1))
                    nc.scalar.activation(pt_hi[:, j, :], turn_ps[:, turn_slot(t, 2 + j), :], ACT.Copy).then_inc(pt_hi_ready, 1)

                if here(t, left):
                    for j in range(min(2, i + 1)):
                        turned_hi(j)
                if here(t + 2, left):
                    u, b, ui = t + 2, (t + 2) // QB % BATCH, (t + 2) % QB
                    act.wait_ge(qkv_ready, ONE(g, u, 1))
                    nc.scalar.activation(squares[:, :, :].rearrange("p h d -> p (h d)"), qkv_flat[:, 0:QK],
                                         ACT.Square).then_inc(squares_ready, 1)
                    nc.scalar.activation(v_hi[:, b, ui, :], v_ps, ACT.Copy).then_inc(v_hi_ready, 1)
                if here(t, left):
                    for j in range(2, i + 1):
                        turned_hi(j)
                if t % BLOCKS == BLOCKS - 3 and here(t + 3, left):
                    split_w(g, g + 1)
                if here(t, left):
                    act.wait_ge(mix_ready, ONE(g, t, 1))
                    nc.scalar.activation(o_hi[:, :], mix_ps[:, :], ACT.Copy).then_inc(o_hi_ready, 1)
                if t % BLOCKS == 0 and here(t, left):
                    if t > 0:
                        act.wait_ge(out_ready, ONE(g, t - 1, 1))
                    split_wo(g + t // BLOCKS)
            pipeline(act, slot)

        @block.vector
        def _(dve):
            for t in range(BLOCKS):
                dve.wait_ge(x_loaded[t], 16)
                nc.vector.bn_stats(bn[:, t, :], x_sb[:, t, :]).then_inc(bn_done, 1)
            for t in range(BLOCKS):
                dve.wait_ge(bn_done, t + 1)
                nc.vector.bn_aggr(moments[:, t, :], bn[:, t, :]).then_inc(moments_done, 1)
            dve.wait_ge(moments_done, BLOCKS)
            nc.vector.tensor_scalar(var_eps[:, :], moments[:, :, 1], LN_EPS, None, ALU.add).then_inc(var_done, 1)
            nc.vector.memset(pt_hi[:, 0:2, :].bitcast(F32), 0.0)
            nc.vector.memset(pt_lo[:, 0:2, :].bitcast(F32), 0.0).then_inc(aw_zeroed, 1)
            dve.wait_ge(rstd_done, 1)
            for t in range(BLOCKS):
                nc.vector.tensor_scalar(x_sb[:, t, :], x_sb[:, t, :], moments[:, t, 0:1], rstd[:, t:t + 1],
                                        ALU.subtract, ALU.mult).then_inc(xn_done, 1)
            for t in range(BLOCKS):
                dve.wait_ge(xt_hi_done, t + 1)
                blk = xt_hi[:, :, t * P:(t + 1) * P]
                nc.vector.tensor_tensor(xt_lo[:, :, t * P:(t + 1) * P],
                                        turn_ps[:, t % 2, :].rearrange("p (c n) -> p c n", c=KC),
                                        blk.bitcast(F32), ALU.subtract).then_inc(xt_lo_done, 1)
            for c in range(KC):
                dve.wait_ge(ffn_hi_done, c + 1)
                nc.vector.tensor_tensor(aw_lo[:, c, 0:LOW + EXPERTS], aw_raw[:, c, :], aw_hi[:, c, 0:LOW + EXPERTS].bitcast(F32),
                                        ALU.subtract).then_inc(ffn_lo_done, 1)
            dve.wait_ge(ffn_hi_done, KC + 1)
            nc.vector.tensor_tensor(bt_lo[:, :], bt_raw, bt_hi[:, :].bitcast(F32), ALU.subtract).then_inc(ffn_lo_done, 1)

            def split_w(group):
                for c in range(KC):
                    dve.wait_ge(w_hi_done, group * KC + (c + 1))
                    nc.vector.tensor_tensor(w_lo[:, c, :], w_raw[:, c, :], w_hi[:, c, :].bitcast(F32),
                                            ALU.subtract).then_inc(w_lo_done, 1)

            def split_wo(group):
                for h in range(HPG):
                    dve.wait_ge(wo_hi_done, group * HPG + (h + 1))
                    nc.vector.tensor_tensor(wo_lo[:, h, :], wo_raw[:, h, :], wo_hi[:, h, :].bitcast(F32),
                                            ALU.subtract).then_inc(wo_lo_done, 1)

            split_w(0)
            dve.wait_ge(small_loaded, 48)
            for t in range(BLOCKS):
                s = t % 2
                dve.wait_ge(low_done, t + 1)
                nc.vector.tensor_tensor(logits[:, s, :], score_ps[:, s, LOW:LOW + EXPERTS], br_sb[:, :], ALU.add).then_inc(logits_done, 1)
                dve.wait_ge(logits_done, t + 1)
                nc.vector.tensor_reduce(logit_max[:, s:s + 1], logits[:, s, :], AX.X, ALU.max, negate=True).then_inc(logit_max_done, 1)
                dve.wait_ge(route_done, t + 1)
                nc.vector.reciprocal(route_inv[:, s:s + 1], route_sum[:, s:s + 1]).then_inc(route_inv_done, 1)
                dve.wait_ge(route_inv_done, t + 1)
                nc.vector.tensor_scalar(route[:, s, :], route[:, s, :], route_inv[:, s:s + 1], FFN_SCALE, ALU.mult, ALU.mult).then_inc(route_scaled, 1)
                dve.wait_ge(route_scaled, t + 1)
                nc.vector.tensor_tensor(low[:, s, :].rearrange("p (e r) -> p e r", e=EXPERTS),
                                        score_ps[:, s, 0:LOW].rearrange("p (e r) -> p e r", e=EXPERTS),
                                        route[:, s, :].unsqueeze(2).broadcast_to([P, EXPERTS, RANK]), ALU.mult).then_inc(low_scaled, 1)
                dve.wait_ge(lt_hi_done, t + 1)
                nc.vector.tensor_tensor(lt_lo[:, s, :], turn_ps[:, s, 0:P], lt_hi[:, s, :].bitcast(F32), ALU.subtract).then_inc(lt_lo_done, 1)
                dve.wait_ge(gate_in_done, t + 1)
                nc.vector.tensor_scalar(sig[:, s, :], gate_ps[s][:, :], EXP_FLOOR, None, ALU.max).then_inc(gate_in_capped, 1)
                dve.wait_ge(gate_exp_done, t + 1)
                nc.vector.tensor_scalar(sig[:, s, :], sig[:, s, :], 1.0, None, ALU.add).then_inc(gate_plus_done, 1)
                dve.wait_ge(gate_plus_done, t + 1)
                nc.vector.reciprocal(sig[:, s, :], sig[:, s, :]).then_inc(gate_recip_done, 1)
                dve.wait_ge(gate_recip_done, t + 1)
                nc.vector.tensor_tensor(gate[:, t, :], gate_ps[s][:, :], sig[:, s, :], ALU.mult).then_inc(gate_done, 1)

            def slot(g, t, left):
                i = t % QB
                n = keys_of(t) * P
                if t % BLOCKS == 0 and here(t, left):
                    if t > 0:
                        dve.wait_ge(biased_ready, PER_HEAD(g, t, 0))
                    col = (g + t // BLOCKS) * HPG
                    nc.vector.tensor_copy(slope[:, :], cst[:, bass.ds(col + C_SLOPE, HPG)]).then_inc(slope_set, 1)
                    dve.wait_ge(slope_set, g + t // BLOCKS + 1)
                if here(t, left):
                    for h in range(HPG):
                        dve.wait_ge(scores_ready, PER_HEAD(g, t, h + 1))
                        dve.sem_inc(scores_taken, 1)
                        first = SEQ - n
                        nc.vector.tensor_tensor_reduce(
                            probs[:, h, 0:n], score_ps[:, h % 2, 0:n], cst[:, C_DIST + first:C_DIST + SEQ],
                            slope[:, h:h + 1], HUGE, ALU.add, ALU.min, neg_max[:, h:h + 1]).then_inc(biased_ready, 1)
                    for h in range(0, HPG, 2):
                        dve.wait_ge(exp_ready, PER_HEAD(g, t, h + 2))
                        nc.vector.reciprocal(recip[:, h:h + 2], total[:, h:h + 2]).then_inc(recip_ready, 1)
                        dve.wait_ge(recip_ready, TWO(g, t, h // 2 + 1))
                        for hh in (h, h + 1):
                            nc.vector.tensor_scalar(probs[:, hh, 0:n], probs[:, hh, 0:n], recip[:, hh:hh + 1], None,
                                                    ALU.mult).then_inc(probs_ready, 1)
                if here(t + 1, left):
                    u, b, ui = t + 1, (t + 1) // QB % BATCH, (t + 1) % QB
                    ks = slice(ui * P, (ui + 1) * P)
                    q_ps, k_ps = turn_ps[:, turn_slot(t, 0), :], turn_ps[:, turn_slot(t, 1), 0:P]
                    if ui > 0:
                        dve.wait_ge(qk_hi_ready, QK_PARTS(g, u, 1))
                        nc.vector.scalar_tensor_tensor(out=q_lo[:, :], in0=q_ps, scalar=qkw_sb[:, 0:1], in1=q_hi[:, :].bitcast(F32),
                                                       op0=ALU.mult, op1=ALU.subtract).then_inc(qk_lo_ready, 1)
                    else:
                        dve.wait_ge(qk_turned, TWO(g, u, 1))
                        nc.vector.tensor_scalar(q_full[:, :], q_ps, qkw_sb[:, 0:1], None, ALU.mult).then_inc(qk_lo_ready, 1)
                    dve.wait_ge(qk_hi_ready, QK_PARTS(g, u, 2 if ui > 0 else 1))
                    if ui == 0:
                        nc.vector.tensor_scalar(k_full[:, :], k_ps, qkw_sb[:, 1:2], None, ALU.mult)
                    nc.vector.scalar_tensor_tensor(out=k_lo[:, b, ks], in0=k_ps, scalar=qkw_sb[:, 1:2], in1=k_hi[:, b, ks].bitcast(F32),
                                                   op0=ALU.mult, op1=ALU.subtract).then_inc(qk_lo_ready, 1)

                def turned_lo(j):
                    dve.wait_ge(pt_hi_ready, PER_KEY_BLOCK(g, t, j + 1))
                    nc.vector.tensor_tensor(pt_lo[:, j, :], turn_ps[:, turn_slot(t, 2 + j), :], pt_hi[:, j, :].bitcast(F32),
                                            ALU.subtract).then_inc(pt_lo_ready, 1)

                if here(t, left):
                    for j in range(min(2, i + 1)):
                        turned_lo(j)
                if here(t + 2, left):
                    u, b, ui = t + 2, (t + 2) // QB % BATCH, (t + 2) % QB
                    if u % BLOCKS == 0:
                        if u > 0:
                            dve.wait_ge(inv_ready, ONE(g, u, 0))
                        col = (g + u // BLOCKS) * NORMED
                        nc.vector.tensor_copy(factor[:, :], cst[:, bass.ds(col + C_FACTOR, NORMED)]).then_inc(factor_set, 1)
                    dve.wait_ge(squares_ready, ONE(g, u, 1))
                    nc.vector.tensor_reduce(sums[:, :], squares[:, :, :], AX.X, ALU.add).then_inc(sums_ready, 1)
                    dve.wait_ge(sums_ready, ONE(g, u, 1))
                    nc.vector.tensor_scalar(mean_sq[:, :], sums[:, :], 1.0 / HD, RMS_EPS, ALU.mult, ALU.add).then_inc(mean_sq_ready, 1)
                    dve.wait_ge(v_hi_ready, ONE(g, u, 1))
                    nc.vector.tensor_tensor(v_lo[:, b, ui, :], v_ps, v_hi[:, b, ui, :].bitcast(F32), ALU.subtract).then_inc(v_lo_ready, 1)
                if here(t, left) and i >= 2:
                    turned_lo(2)
                if here(t + 2, left):
                    dve.wait_ge(inv_rms_ready, ONE(g, u, 1))
                    dve.wait_ge(factor_set, g + u // BLOCKS + 1)
                    nc.vector.tensor_tensor(inv[:, :], inv_rms[:, :], factor[:, :], ALU.mult).then_inc(inv_ready, 1)
                    dve.wait_ge(inv_ready, ONE(g, u, 1))
                    nc.vector.tensor_tensor(qk_norm[:, :, :], qkv_flat[:, 0:QK].rearrange("p (h d) -> p h d", h=NORMED),
                                            inv[:, :].unsqueeze(2).broadcast_to([P, NORMED, HD]), ALU.mult).then_inc(qk_norm_ready, 1)
                if here(t, left) and i >= 3:
                    turned_lo(3)
                if t % BLOCKS == BLOCKS - 3 and here(t + 3, left):
                    split_w(g + 1)
                if here(t - 1, left):
                    add_out(g, t - 1, left)
                if here(t, left):
                    dve.wait_ge(o_hi_ready, ONE(g, t, 1))
                    nc.vector.tensor_tensor(o_lo[:, :], mix_ps[:, :], o_hi[:, :].bitcast(F32), ALU.subtract).then_inc(o_lo_ready, 1)
                if t % BLOCKS == 0 and here(t, left):
                    split_wo(g + t // BLOCKS)

            def add_out(g, t, left):
                m = t % BLOCKS
                dve.wait_ge(out_ready, ONE(g, t, 1))
                nc.vector.tensor_tensor(acc[:, m, :], out_ps[:, :], acc[:, m, :], ALU.add).then_inc(acc_ready, 1)
                if left == 1:
                    dve.wait_ge(acc_ready, 1 + ONE(g, t, 1))
                    nc.vector.tensor_tensor(acc[:, m, :], acc[:, m, :], gate[:, m, :], ALU.mult).then_inc(gated_ready, 1)
                    dve.wait_ge(gated_ready, m + 1)
                    nc.vector.tensor_tensor(acc[:, m, :], acc[:, m, :], x_sb[:, m, :], ALU.add).then_inc(y_ready, 1)

            dve.wait_ge(acc_ready, 1)
            dve.wait_ge(x_again, 16)
            pipeline(dve, slot)

        @block.tensor
        def _(pe):
            def three(out, a_hi, a_lo, b_hi, b_lo, start, stop):
                pe.matmul(out, a_hi, b_hi, start=start, stop=False)
                pe.matmul(out, a_hi, b_lo, start=False, stop=False)
                return pe.matmul(out, a_lo, b_hi, start=False, stop=stop)

            def project(g, t):
                m = t % BLOCKS
                rows = slice(m * P, (m + 1) * P)
                if t > 0:
                    pe.wait_ge(qk_norm_ready, ONE(g, t - 1, 1))
                    pe.wait_ge(v_lo_ready, ONE(g, t - 1, 1))
                for c in range(KC):
                    if m == 0:
                        pe.wait_ge(w_lo_done, (g + t // BLOCKS) * KC + (c + 1))
                    for bank, lo, hi in ((0, 0, QW), (1, QW, QKV)):
                        last = three(qkv_ps[:, bank, 0:hi - lo], xt_hi[:, c, rows], xt_lo[:, c, rows],
                                     w_hi[:, c, lo:hi], w_lo[:, c, lo:hi], c == 0, c == KC - 1)
                last.then_inc(qkv_ready, 1)

            pe.wait_ge(small_loaded, 48)
            for t in range(BLOCKS):
                pe.wait_ge(xn_done, t + 1)
                if t >= 2:
                    pe.wait_ge(xt_lo_done, t - 1)
                for c in range(KC):
                    tr = pe.transpose(turn_ps[:, t % 2, c * P:(c + 1) * P], x_sb[:, t, c * P:(c + 1) * P], ident)
                tr.then_inc(xt_turned, 1)
            pe.wait_ge(ffn_lo_done, KC + 1)
            pe.wait_ge(xt_lo_done, BLOCKS)
            for t in range(BLOCKS):
                s = t % 2
                if t >= 2:
                    pe.wait_ge(low_scaled, t - 1)
                for c in range(KC):
                    last = three(score_ps[:, s, 0:AW], xt_hi[:, c, t * P:(t + 1) * P], xt_lo[:, c, t * P:(t + 1) * P],
                                 aw_hi[:, c, :], aw_lo[:, c, :], c == 0, c == KC - 1)
                last.then_inc(low_done, 1)
                pe.wait_ge(low_scaled, t + 1)
                if t >= 2:
                    pe.wait_ge(lt_lo_done, t - 1)
                pe.transpose(turn_ps[:, s, 0:P], low[:, s, :], ident).then_inc(low_turned, 1)
                pe.wait_ge(lt_lo_done, t + 1)
                if t >= 2:
                    pe.wait_ge(gate_done, t - 1)
                three(gate_ps[s][:, :], lt_hi[:, s, :], lt_lo[:, s, :], bt_hi[:, :], bt_lo[:, :], True, True).then_inc(gate_in_done, 1)
            pe.wait_ge(gate_done, BLOCKS)

            def slot(g, t, left):
                i, b = t % QB, t // QB % BATCH
                n = keys_of(t) * P
                if here(t, left):
                    pe.wait_ge(qk_lo_ready, TWO(g, t, 2))
                    for h in range(HPG):
                        if t > 0 or h >= 2:
                            pe.wait_ge(biased_ready, PER_HEAD(g, t, h - 1))
                        hs = slice(h * HD, (h + 1) * HD)
                        out = score_ps[:, h % 2, 0:n]
                        if i == 0:
                            last = pe.matmul(out, q_full[:, hs], k_full[:, :], start=True, stop=True)
                        else:
                            last = three(out, q_hi[:, hs], q_lo[:, hs], k_hi[:, b, 0:n], k_lo[:, b, 0:n], True, True)
                        last.then_inc(scores_ready, 1)
                if here(t + 1, left):
                    u = t + 1
                    pe.wait_ge(qk_norm_ready, ONE(g, u, 1))
                    if t > 0:
                        if (t - 1) % QB == 0:
                            pe.wait_ge(qk_lo_ready, TWO(g, t, 2))
                        pe.wait_ge(pt_lo_ready, PER_KEY_BLOCK(g, t, 0))
                    for h in range(HPG):
                        tr = pe.transpose(turn_ps[:, turn_slot(t, 0), h * P:(h + 1) * P], qk_norm[:, h, :], ident)
                    tr.then_inc(qk_turned, 1)
                    pe.transpose(turn_ps[:, turn_slot(t, 1), 0:P], qk_norm[:, HPG, :], ident).then_inc(qk_turned, 1)
                if here(t + 2, left):
                    project(g, t + 2)

                def turn_probs(j):
                    if j >= 2:
                        pe.wait_ge(pt_lo_ready, PER_KEY_BLOCK(g, t, j - 1))
                    elif here(t + 1, left):
                        pe.wait_ge(qk_lo_ready, TWO(g, t + 1, j + 1))
                    else:
                        pe.wait_ge(pt_lo_ready, PER_KEY_BLOCK(g, t, 0))
                    if j == 0:
                        pe.wait_ge(probs_ready, PER_HEAD(g, t, HPG))
                    for h in range(HPG):
                        tr = pe.transpose(turn_ps[:, turn_slot(t, 2 + j), h * P:(h + 1) * P], probs[:, h, j * P:(j + 1) * P], ident)
                    tr.then_inc(probs_turned, 1)

                def mix(j):
                    pe.wait_ge(pt_lo_ready, PER_KEY_BLOCK(g, t, j + 1))
                    if j == 0:
                        pe.wait_ge(v_lo_ready, ONE(g, t, 1))
                        if t > 0:
                            pe.wait_ge(o_lo_ready, ONE(g, t - 1, 1))
                    last = three(mix_ps[:, :], v_hi[:, b, j, :], v_lo[:, b, j, :], pt_hi[:, j, :], pt_lo[:, j, :], j == 0, j == i)
                    if j == i:
                        last.then_inc(mix_ready, 1)

                def out(half):
                    if t == 0:
                        return
                    if half == 0:
                        pe.wait_ge(o_lo_ready, ONE(g, t - 1, 1))
                        pe.wait_ge(acc_ready, 1 + ONE(g, t - 2, 1))
                        if (t - 1) % BLOCKS == 0:
                            pe.wait_ge(wo_lo_done, (g + (t - 1) // BLOCKS) * HPG + HPG)
                    for h in range(half * 2, half * 2 + 2):
                        hs = slice(h * P, (h + 1) * P)
                        last = three(out_ps[:, :], o_hi[:, hs], o_lo[:, hs], wo_hi[:, h, :], wo_lo[:, h, :], h == 0, h == HPG - 1)
                    if half == 1:
                        last.then_inc(out_ready, 1)

                if here(t, left):
                    turn_probs(0)
                    if i >= 1:
                        turn_probs(1)
                    out(0)
                    if i >= 1:
                        mix(0)
                    for j in range(2, i + 1):
                        turn_probs(j)
                        if j < i:
                            mix(j - 1)
                    out(1)
                    for j in range(max(i - 1, 0) if i >= 1 else 0, i + 1):
                        if i >= 1 and j == 0:
                            continue
                        mix(j)
                elif here(t - 1, left):
                    out(0)
                    out(1)
            pipeline(pe, slot)


def kernel(L0_attn_x, L0_attn_Wq, L0_attn_Wk, L0_attn_Wv, L0_attn_Wo, L0_attn_q_norm_w, L0_attn_k_norm_w,
           L0_ffn_A, L0_ffn_B, L0_ffn_Wr, L0_ffn_br):
    import concourse.bacc as bacc
    from concourse.bass_utils import run_bass_kernel_spmd

    def by_group(w, heads):
        return np.asarray(w).reshape(GROUPS, heads * HD, KC, P).transpose(0, 3, 2, 1)

    wqkv = np.concatenate([by_group(L0_attn_Wq, HPG), by_group(L0_attn_Wk, 1), by_group(L0_attn_Wv, 1)], axis=3)
    wo = np.asarray(L0_attn_Wo).reshape(DM, GROUPS, HPG, HD).transpose(1, 3, 2, 0)
    aw = np.concatenate([np.asarray(L0_ffn_A).reshape(LOW, DM), np.asarray(L0_ffn_Wr)], axis=0)
    aw = aw.reshape(LOW + EXPERTS, KC, P).transpose(2, 1, 0)
    arrays = {
        "x": np.asarray(L0_attn_x).reshape(BLOCKS * P, DM),
        "wqkv": wqkv.reshape(GROUPS, P, KC * QKV),
        "wo": wo.reshape(GROUPS, P, HPG * DM),
        "aw": aw.reshape(P, KC * (LOW + EXPERTS)),
        "bt": np.asarray(L0_ffn_B).transpose(0, 2, 1).reshape(LOW, DM),
        "br": np.broadcast_to(np.asarray(L0_ffn_br), (P, EXPERTS)),
        "qkw": np.stack([np.asarray(L0_attn_q_norm_w), np.asarray(L0_attn_k_norm_w)], axis=1),
        "consts": constants(),
    }
    arrays = {name: np.ascontiguousarray(a) for name, a in arrays.items()}
    nc = bacc.Bacc("TRN2", target_bir_lowering=False, num_devices=1)
    args = [nc.dram_tensor(name, a.shape, mybir.dt.from_np(a.dtype), kind="ExternalInput").ap() for name, a in arrays.items()]
    y = nc.dram_tensor("y", (BLOCKS * P, DM), F32, kind="ExternalOutput").ap()
    build(nc, *args, y)
    r = run_bass_kernel_spmd(nc, [arrays], core_ids=[0])
    return r.results[0]["y"].reshape(BATCH, SEQ, DM)
```

```python
from contextlib import ExitStack

import numpy as np

import concourse.bass as bass
from concourse import mybir

F32 = mybir.dt.float32
F32R = mybir.dt.float32r
ALU = mybir.AluOpType
ACT = mybir.ActivationFunctionType
AX = mybir.AxisListType

P = 128
BATCH, SEQ, DM = 2, 512, 512
HEADS, GROUPS, HD = 32, 8, 128
HPG = HEADS // GROUPS
QB = SEQ // P
BLOCKS = BATCH * QB
UNITS = GROUPS * BLOCKS
KC = DM // P
QW = HPG * HD
NORMED = HPG + 1
QK = NORMED * HD
QKV = QK + HD
EXPERTS, RANK = 8, 16
LOW = EXPERTS * RANK
AW = 256
FFN_SCALE = 2.0 * EXPERTS
LN_EPS, RMS_EPS = 1e-5, 1e-6
MASKED = 1e30
HUGE = 3e38

C_IDENT = 0
C_DIST = C_IDENT + P
C_SLOPE = C_DIST + SEQ
C_FACTOR = C_SLOPE + HEADS
C_END = C_FACTOR + GROUPS * NORMED


def constants():
    import math
    start = 2 ** (-2 ** (-(math.log2(HEADS) - 3)))
    slopes = np.array([start * start ** i for i in range(HEADS)], dtype=np.float32)
    c = np.zeros((P, C_END), np.float32)
    c[:, C_IDENT:C_DIST] = np.eye(P)
    d = np.arange(P)[:, None] + (SEQ - P) - np.arange(SEQ)[None, :]
    c[:, C_DIST:C_SLOPE] = np.where(d < 0, MASKED, d)
    c[:, C_SLOPE:C_FACTOR] = slopes
    f = np.ones((GROUPS, NORMED))
    f[:, :HPG] = -1.0 / (slopes.astype(np.float64).reshape(GROUPS, HPG) * math.sqrt(HD))
    c[:, C_FACTOR:] = f.reshape(1, -1)
    return c


def counter(per_unit):
    n = len(per_unit)

    def value(g, t, e):
        return g * sum(per_unit) + (t // n) * sum(per_unit) + sum(per_unit[:t % n]) + e
    return value


ONE = counter([1] * BLOCKS)
TWO = counter([2] * BLOCKS)
PER_HEAD = counter([HPG] * BLOCKS)
PER_KEY_BLOCK = counter([i + 1 for i in range(QB)] * BATCH)
QK_PARTS = counter(([1] + [2] * (QB - 1)) * BATCH)


def keys_of(t):
    return t % QB + 1


def build(nc, x, wqkv, wo, aw, bt, br, qkw, consts, y):
    with ExitStack() as ctx:
        def sb(name, shape, dt=F32):
            return ctx.enter_context(nc.sbuf_tensor(name, [P, *shape], dt))

        def psum(name, shape):
            return ctx.enter_context(nc.psum_tensor(name, [P, *shape], F32))

        def sem(name):
            return ctx.enter_context(nc.semaphore(name))

        cst = sb("cst", [C_END])
        ident = cst[:, C_IDENT:C_DIST]
        qkw_sb = sb("qkw_sb", [2])
        br_sb = sb("br_sb", [EXPERTS])
        x_sb = sb("x_sb", [BLOCKS, DM])
        xt_hi, xt_lo = (sb(f"xt_{p}", [KC, BLOCKS * P], F32R) for p in ("hi", "lo"))
        w_raw = sb("w_raw", [KC, QKV])
        w_hi, w_lo = (sb(f"w_{p}", [KC, QKV], F32R) for p in ("hi", "lo"))
        wo_raw = sb("wo_raw", [HPG, DM])
        wo_hi, wo_lo = (sb(f"wo_{p}", [HPG, DM], F32R) for p in ("hi", "lo"))
        bt_hi, bt_lo = (sb(f"bt_{p}", [DM], F32R) for p in ("hi", "lo"))
        squares = sb("squares", [NORMED, HD])
        qk_norm = sb("qk_norm", [NORMED, HD])
        q_full = sb("q_full", [QW])
        k_full = sb("k_full", [P])
        q_hi, q_lo = (sb(f"q_{p}", [QW], F32R) for p in ("hi", "lo"))
        k_hi, k_lo = (sb(f"k_{p}", [BATCH, SEQ], F32R) for p in ("hi", "lo"))
        v_hi, v_lo = (sb(f"v_{p}", [BATCH, QB, HD], F32R) for p in ("hi", "lo"))
        probs = sb("probs", [HPG, SEQ])
        pt_hi, pt_lo = (sb(f"pt_{p}", [QB, HPG * P], F32R) for p in ("hi", "lo"))
        o_hi, o_lo = (sb(f"o_{p}", [HPG * P], F32R) for p in ("hi", "lo"))
        acc = sb("acc", [BLOCKS, DM])
        gate = sb("gate", [BLOCKS, DM])
        slope = sb("slope", [HPG])
        factor = sb("factor", [NORMED])
        sums = sb("sums", [NORMED])
        mean_sq = sb("mean_sq", [NORMED])
        inv_rms = sb("inv_rms", [NORMED])
        inv = sb("inv", [NORMED])
        minus_half = sb("minus_half", [8])
        neg_max = sb("neg_max", [HPG])
        total = sb("total", [HPG])
        recip = sb("recip", [HPG])
        bn = sb("bn", [BLOCKS, 6])
        moments = sb("moments", [BLOCKS, 2])
        var_eps = sb("var_eps", [BLOCKS])
        rstd = sb("rstd", [BLOCKS])
        logits = sb("logits", [2, EXPERTS])
        logit_max = sb("logit_max", [2])
        route = sb("route", [2, EXPERTS])
        route_sum = sb("route_sum", [2])
        route_inv = sb("route_inv", [2])
        low = probs[:, 0, 0:2 * LOW].rearrange("p (s l) -> p s l", s=2)
        aw_raw = sb("aw_raw", [KC, LOW + EXPERTS])
        aw_hi = pt_hi[:, 0:2, :].rearrange("p a (b n) -> p (a b) n", b=2)
        aw_lo = pt_lo[:, 0:2, :].rearrange("p a (b n) -> p (a b) n", b=2)
        lt_hi = pt_hi[:, 2, 0:2 * P].rearrange("p (s n) -> p s n", s=2)
        lt_lo = pt_lo[:, 2, 0:2 * P].rearrange("p (s n) -> p s n", s=2)
        bt_raw = squares[:, 0:HPG, :].rearrange("p a n -> p (a n)")

        qkv_ps = psum("qkv_ps", [2, 512])
        score_ps = psum("score_ps", [2, 512])
        turn_ps = psum("turn_ps", [2, 512])
        mix_ps = psum("mix_ps", [512])
        out_ps = psum("out_ps", [512])
        qkv_flat = qkv_ps[:, :, :].rearrange("p a n -> p (a n)")
        v_ps = qkv_flat[:, QK:QKV]
        gate_ps = [mix_ps, out_ps]

        x_loaded = [sem(f"x_loaded{t}") for t in range(BLOCKS)]
        small_loaded = sem("small_loaded")
        ffn_loaded = sem("ffn_loaded")
        w_loaded = sem("w_loaded")
        wo_loaded = sem("wo_loaded")
        x_again = sem("x_again")
        stored = sem("stored")
        half_set = sem("half_set")
        bn_done = sem("bn_done")
        moments_done = sem("moments_done")
        var_done = sem("var_done")
        rstd_done = sem("rstd_done")
        xn_done = sem("xn_done")
        xt_turned = sem("xt_turned")
        xt_hi_done = sem("xt_hi_done")
        xt_lo_done = sem("xt_lo_done")
        aw_zeroed = sem("aw_zeroed")
        ffn_hi_done = sem("ffn_hi_done")
        ffn_lo_done = sem("ffn_lo_done")
        low_done = sem("low_done")
        logits_done = sem("logits_done")
        logit_max_done = sem("logit_max_done")
        route_done = sem("route_done")
        route_inv_done = sem("route_inv_done")
        route_scaled = sem("route_scaled")
        low_scaled = sem("low_scaled")
        low_turned = sem("low_turned")
        lt_hi_done = sem("lt_hi_done")
        lt_lo_done = sem("lt_lo_done")
        gate_in_done = sem("gate_in_done")
        gate_in_kept = sem("gate_in_kept")
        gate_done = sem("gate_done")
        w_hi_done = sem("w_hi_done")
        w_lo_done = sem("w_lo_done")
        wo_hi_done = sem("wo_hi_done")
        wo_lo_done = sem("wo_lo_done")
        slope_set = sem("slope_set")
        factor_set = sem("factor_set")
        qkv_ready = sem("qkv_ready")
        squares_ready = sem("squares_ready")
        sums_ready = sem("sums_ready")
        mean_sq_ready = sem("mean_sq_ready")
        inv_rms_ready = sem("inv_rms_ready")
        inv_ready = sem("inv_ready")
        qk_norm_ready = sem("qk_norm_ready")
        v_hi_ready = sem("v_hi_ready")
        v_lo_ready = sem("v_lo_ready")
        qk_turned = sem("qk_turned")
        qk_hi_ready = sem("qk_hi_ready")
        qk_lo_ready = sem("qk_lo_ready")
        scores_ready = sem("scores_ready")
        scores_taken = sem("scores_taken")
        biased_ready = sem("biased_ready")
        exp_ready = sem("exp_ready")
        recip_ready = sem("recip_ready")
        probs_ready = sem("probs_ready")
        probs_turned = sem("probs_turned")
        pt_hi_ready = sem("pt_hi_ready")
        pt_lo_ready = sem("pt_lo_ready")
        mix_ready = sem("mix_ready")
        o_hi_ready = sem("o_hi_ready")
        o_lo_ready = sem("o_lo_ready")
        out_ready = sem("out_ready")
        acc_ready = sem("acc_ready")
        gated_ready = sem("gated_ready")
        y_ready = sem("y_ready")

        def turn_slot(s, n):
            per = [keys_of(i) + 2 for i in range(QB)]
            return (sum(per) * (s // QB) + sum(per[:s % QB]) + n) % 2

        def pipeline(eng, slot):
            for t in range(-2, 2):
                slot(0, t, GROUPS)
            with eng.Fori(0, GROUPS - 1) as g:
                for t in range(2, BLOCKS + 2):
                    slot(g, t, GROUPS)
            for t in range(2, BLOCKS + 2):
                slot(GROUPS - 1, t, 1)

        def here(t, left):
            return 0 <= t < BLOCKS * left

        block = ctx.enter_context(nc.Block())

        @block.sync
        def _(sp):
            for t in range(BLOCKS):
                sp.dma_start(x_sb[:, t, :], x[t * P:(t + 1) * P, :]).then_inc(x_loaded[t], 16)
            sp.dma_start(aw_raw[:, :, :].rearrange("p c n -> p (c n)"), aw).then_inc(ffn_loaded, 16)
            sp.dma_start(bt_raw, bt).then_inc(ffn_loaded, 16)
            sp.dma_start(wo_raw[:, :, :].rearrange("p c n -> p (c n)"), wo[0:1].rearrange("a p n -> p (a n)")).then_inc(wo_loaded, 16)
            sp.wait_ge(xt_turned, BLOCKS)
            sp.dma_start(x_sb[:, :, :], x.rearrange("(t p) n -> p t n", p=P)).then_inc(x_again, 16)
            with sp.Fori(0, GROUPS - 1) as g:
                sp.wait_ge(w_lo_done, g * KC + KC)
                sp.dma_start(w_raw[:, :, :].rearrange("p c n -> p (c n)"), wqkv[bass.ds(g + 1, 1)].rearrange("a p n -> p (a n)")).then_inc(w_loaded, 16)
                sp.wait_ge(wo_lo_done, g * HPG + HPG)
                sp.dma_start(wo_raw[:, :, :].rearrange("p c n -> p (c n)"), wo[bass.ds(g + 1, 1)].rearrange("a p n -> p (a n)")).then_inc(wo_loaded, 16)
            for t in range(BLOCKS):
                sp.wait_ge(y_ready, t + 1)
                sp.dma_start(y[t * P:(t + 1) * P, :], acc[:, t, :]).then_inc(stored, 16)
            sp.wait_ge(stored, 16 * BLOCKS)

        @block.gpsimd
        def _(pool):
            nc.gpsimd.memset(minus_half[:, :], -0.5).then_inc(half_set, 1)
            nc.gpsimd.memset(acc[:, :, :], 0.0).then_inc(acc_ready, 1)
            pool.wait_ge(half_set, 1)
            for t in range(BLOCKS):
                pool.wait_ge(var_done, t + 1)
                nc.gpsimd.tensor_tensor(rstd[:, t:t + 1], var_eps[:, t:t + 1], minus_half[:, 0:1], ALU.pow).then_inc(rstd_done, 1)

            def split_w(group):
                for c in range(KC):
                    pool.wait_ge(w_hi_done, group * KC + (c + 1))
                    nc.gpsimd.tensor_tensor(w_lo[:, c, :], w_raw[:, c, :], w_hi[:, c, :].bitcast(F32),
                                            ALU.subtract).then_inc(w_lo_done, 1)

            def split_wo(group):
                for h in range(HPG):
                    pool.wait_ge(wo_hi_done, group * HPG + (h + 1))
                    nc.gpsimd.tensor_tensor(wo_lo[:, h, :], wo_raw[:, h, :], wo_hi[:, h, :].bitcast(F32),
                                            ALU.subtract).then_inc(wo_lo_done, 1)

            split_w(0)

            def slot(g, t, left):
                if here(t + 2, left):
                    pool.wait_ge(mean_sq_ready, ONE(g, t + 2, 1))
                    nc.gpsimd.tensor_tensor(inv_rms[:, :], mean_sq[:, :], minus_half[:, 0:NORMED],
                                            ALU.pow).then_inc(inv_rms_ready, 1)
                if t % BLOCKS == BLOCKS - 3 and here(t + 3, left):
                    split_w(g + 1)
                if t % BLOCKS == 0 and here(t, left):
                    split_wo(g + t // BLOCKS)
            pipeline(pool, slot)

        @block.scalar
        def _(act):
            act.dma_start(cst[:, :], consts).then_inc(small_loaded, 16)
            act.dma_start(qkw_sb[:, :], qkw).then_inc(small_loaded, 16)
            act.dma_start(br_sb[:, :], br).then_inc(small_loaded, 16)
            act.dma_start(w_raw[:, :, :].rearrange("p c n -> p (c n)"), wqkv[0:1].rearrange("a p n -> p (a n)")).then_inc(w_loaded, 16)

            def split_w(group):
                act.wait_ge(w_loaded, group * 16 + 16)
                for c in range(KC):
                    nc.scalar.activation(w_hi[:, c, :], w_raw[:, c, :], ACT.Copy).then_inc(w_hi_done, 1)

            def split_wo(group):
                act.wait_ge(wo_loaded, group * 16 + 16)
                for h in range(HPG):
                    nc.scalar.activation(wo_hi[:, h, :], wo_raw[:, h, :], ACT.Copy).then_inc(wo_hi_done, 1)

            for t in range(BLOCKS):
                act.wait_ge(xt_turned, t + 1)
                nc.scalar.activation(xt_hi[:, :, t * P:(t + 1) * P],
                                     turn_ps[:, t % 2, :].rearrange("p (c n) -> p c n", c=KC),
                                     ACT.Copy).then_inc(xt_hi_done, 1)
            act.wait_ge(ffn_loaded, 32)
            act.wait_ge(aw_zeroed, 1)
            nc.scalar.activation(aw_hi[:, :, 0:LOW + EXPERTS], aw_raw[:, :, :], ACT.Copy).then_inc(ffn_hi_done, 1)
            nc.scalar.activation(bt_hi[:, :], bt_raw, ACT.Copy).then_inc(ffn_hi_done, 1)
            split_w(0)
            for k in range(BLOCKS + 2):
                if k < BLOCKS:
                    s = k % 2
                    act.wait_ge(logit_max_done, k + 1)
                    nc.scalar.activation(route[:, s, :], logits[:, s, :], ACT.Exp, bias=logit_max[:, s:s + 1],
                                         accum_out=route_sum[:, s:s + 1]).then_inc(route_done, 1)
                if 1 <= k <= BLOCKS:
                    t = k - 1
                    act.wait_ge(low_turned, t + 1)
                    nc.scalar.activation(lt_hi[:, t % 2, :], turn_ps[:, t % 2, 0:P], ACT.Copy).then_inc(lt_hi_done, 1)
                if k >= 2:
                    t = k - 2
                    act.wait_ge(gate_in_done, t + 1)
                    nc.scalar.activation(gate[:, t, :], gate_ps[t % 2][:, :], ACT.Copy).then_inc(gate_in_kept, 1)
            act.wait_ge(gate_in_kept, BLOCKS)
            for t in range(0, BLOCKS, BLOCKS // 2):
                nc.scalar.activation(gate[:, t:t + BLOCKS // 2, :], gate[:, t:t + BLOCKS // 2, :], ACT.Silu).then_inc(gate_done, 1)

            def slot(g, t, left):
                i = t % QB
                n = keys_of(t) * P

                def exponentials(heads):
                    for h in heads:
                        act.wait_ge(biased_ready, PER_HEAD(g, t, h + 1))
                        nc.scalar.activation(probs[:, h, 0:n], probs[:, h, 0:n], ACT.Exp, bias=neg_max[:, h:h + 1],
                                             scale=-1.0, accum_out=total[:, h:h + 1]).then_inc(exp_ready, 1)

                def turned_hi(j):
                    act.wait_ge(probs_turned, PER_KEY_BLOCK(g, t, j + 1))
                    nc.scalar.activation(pt_hi[:, j, :], turn_ps[:, turn_slot(t, 2 + j), :], ACT.Copy).then_inc(pt_hi_ready, 1)

                if here(t, left):
                    exponentials(range(0, 2))
                if here(t - 1, left):
                    act.wait_ge(mix_ready, ONE(g, t - 1, 1))
                    nc.scalar.activation(o_hi[:, :], mix_ps[:, :], ACT.Copy).then_inc(o_hi_ready, 1)
                if here(t, left):
                    exponentials(range(2, HPG))
                if here(t + 1, left):
                    u, b, ui = t + 1, (t + 1) // QB % BATCH, (t + 1) % QB
                    if ui > 0:
                        act.wait_ge(qk_turned, TWO(g, u, 1))
                        nc.scalar.activation(q_hi[:, :], turn_ps[:, turn_slot(t, 0), :], ACT.Copy,
                                             scale=qkw_sb[:, 0:1]).then_inc(qk_hi_ready, 1)
                    act.wait_ge(qk_turned, TWO(g, u, 2))
                    nc.scalar.activation(k_hi[:, b, ui * P:(ui + 1) * P], turn_ps[:, turn_slot(t, 1), 0:P], ACT.Copy,
                                         scale=qkw_sb[:, 1:2]).then_inc(qk_hi_ready, 1)
                if here(t + 2, left):
                    u, b, ui = t + 2, (t + 2) // QB % BATCH, (t + 2) % QB
                    act.wait_ge(qkv_ready, ONE(g, u, 1))
                    nc.scalar.activation(squares[:, :, :].rearrange("p h d -> p (h d)"), qkv_flat[:, 0:QK],
                                         ACT.Square).then_inc(squares_ready, 1)
                if here(t, left):
                    for j in range(min(2, i + 1)):
                        turned_hi(j)
                if here(t + 2, left):
                    nc.scalar.activation(v_hi[:, b, ui, :], v_ps, ACT.Copy).then_inc(v_hi_ready, 1)
                if here(t, left):
                    for j in range(2, i + 1):
                        turned_hi(j)
                if t % BLOCKS == BLOCKS - 3 and here(t + 3, left):
                    split_w(g + 1)
                if t % BLOCKS == 0 and here(t, left):
                    if t > 0:
                        act.wait_ge(out_ready, ONE(g, t - 1, 1))
                    split_wo(g + t // BLOCKS)
            pipeline(act, slot)

        @block.vector
        def _(dve):
            nc.vector.memset(pt_hi[:, 0:2, :].bitcast(F32), 0.0)
            nc.vector.memset(pt_lo[:, 0:2, :].bitcast(F32), 0.0).then_inc(aw_zeroed, 1)
            for k in range(BLOCKS + 3):
                if k < BLOCKS:
                    dve.wait_ge(x_loaded[k], 16)
                    nc.vector.bn_stats(bn[:, k, :], x_sb[:, k, :]).then_inc(bn_done, 1)
                    dve.wait_ge(bn_done, k + 1)
                    nc.vector.bn_aggr(moments[:, k, :], bn[:, k, :]).then_inc(moments_done, 1)
                    dve.wait_ge(moments_done, k + 1)
                    nc.vector.tensor_scalar(var_eps[:, k:k + 1], moments[:, k, 1:2], LN_EPS, None, ALU.add).then_inc(var_done, 1)
                if 2 <= k < BLOCKS + 2:
                    t = k - 2
                    dve.wait_ge(rstd_done, t + 1)
                    nc.vector.tensor_scalar(x_sb[:, t, :], x_sb[:, t, :], moments[:, t, 0:1], rstd[:, t:t + 1],
                                            ALU.subtract, ALU.mult).then_inc(xn_done, 1)
                if k >= 3:
                    t = k - 3
                    dve.wait_ge(xt_hi_done, t + 1)
                    nc.vector.tensor_tensor(xt_lo[:, :, t * P:(t + 1) * P],
                                            turn_ps[:, t % 2, :].rearrange("p (c n) -> p c n", c=KC),
                                            xt_hi[:, :, t * P:(t + 1) * P].bitcast(F32), ALU.subtract).then_inc(xt_lo_done, 1)
            dve.wait_ge(ffn_hi_done, 2)
            nc.vector.tensor_tensor(aw_lo[:, :, 0:LOW + EXPERTS], aw_raw[:, :, :], aw_hi[:, :, 0:LOW + EXPERTS].bitcast(F32),
                                    ALU.subtract).then_inc(ffn_lo_done, 1)
            nc.vector.tensor_tensor(bt_lo[:, :], bt_raw, bt_hi[:, :].bitcast(F32), ALU.subtract).then_inc(ffn_lo_done, 1)
            dve.wait_ge(small_loaded, 48)
            for k in range(BLOCKS + 1):
                s = k % 2
                if k < BLOCKS:
                    dve.wait_ge(low_done, k + 1)
                    nc.vector.tensor_tensor(logits[:, s, :], score_ps[:, s, LOW:LOW + EXPERTS], br_sb[:, :], ALU.add).then_inc(logits_done, 1)
                    dve.wait_ge(logits_done, k + 1)
                    nc.vector.tensor_reduce(logit_max[:, s:s + 1], logits[:, s, :], AX.X, ALU.max, negate=True).then_inc(logit_max_done, 1)
                if k >= 1:
                    t = k - 1
                    dve.wait_ge(lt_hi_done, t + 1)
                    nc.vector.tensor_tensor(lt_lo[:, t % 2, :], turn_ps[:, t % 2, 0:P], lt_hi[:, t % 2, :].bitcast(F32),
                                            ALU.subtract).then_inc(lt_lo_done, 1)
                if k < BLOCKS:
                    dve.wait_ge(route_done, k + 1)
                    nc.vector.reciprocal(route_inv[:, s:s + 1], route_sum[:, s:s + 1]).then_inc(route_inv_done, 1)
                    dve.wait_ge(route_inv_done, k + 1)
                    nc.vector.tensor_scalar(route[:, s, :], route[:, s, :], route_inv[:, s:s + 1], FFN_SCALE, ALU.mult, ALU.mult).then_inc(route_scaled, 1)
                    dve.wait_ge(route_scaled, k + 1)
                    nc.vector.tensor_tensor(low[:, s, :].rearrange("p (e r) -> p e r", e=EXPERTS),
                                            score_ps[:, s, 0:LOW].rearrange("p (e r) -> p e r", e=EXPERTS),
                                            route[:, s, :].unsqueeze(2).broadcast_to([P, EXPERTS, RANK]), ALU.mult).then_inc(low_scaled, 1)

            def slot(g, t, left):
                i = t % QB
                n = keys_of(t) * P
                if t % BLOCKS == 0 and here(t, left):
                    if t > 0:
                        dve.wait_ge(biased_ready, PER_HEAD(g, t, 0))
                    col = (g + t // BLOCKS) * HPG
                    nc.vector.tensor_copy(slope[:, :], cst[:, bass.ds(col + C_SLOPE, HPG)]).then_inc(slope_set, 1)
                    dve.wait_ge(slope_set, g + (t // BLOCKS + 1))
                if here(t, left):
                    for h in range(HPG):
                        dve.wait_ge(scores_ready, PER_HEAD(g, t, h + 1))
                        dve.sem_inc(scores_taken, 1)
                        nc.vector.tensor_tensor_reduce(
                            probs[:, h, 0:n], score_ps[:, h % 2, 0:n], cst[:, C_DIST + SEQ - n:C_DIST + SEQ],
                            slope[:, h:h + 1], HUGE, ALU.add, ALU.min, neg_max[:, h:h + 1]).then_inc(biased_ready, 1)
                    for h in range(0, HPG, 2):
                        dve.wait_ge(exp_ready, PER_HEAD(g, t, h + 2))
                        nc.vector.reciprocal(recip[:, h:h + 2], total[:, h:h + 2]).then_inc(recip_ready, 1)
                        dve.wait_ge(recip_ready, TWO(g, t, h // 2 + 1))
                        for hh in (h, h + 1):
                            nc.vector.tensor_scalar(probs[:, hh, 0:n], probs[:, hh, 0:n], recip[:, hh:hh + 1], None,
                                                    ALU.mult).then_inc(probs_ready, 1)
                if here(t + 1, left):
                    u, b, ui = t + 1, (t + 1) // QB % BATCH, (t + 1) % QB
                    ks = slice(ui * P, (ui + 1) * P)
                    q_ps, k_ps = turn_ps[:, turn_slot(t, 0), :], turn_ps[:, turn_slot(t, 1), 0:P]
                    if ui > 0:
                        dve.wait_ge(qk_hi_ready, QK_PARTS(g, u, 1))
                        nc.vector.scalar_tensor_tensor(out=q_lo[:, :], in0=q_ps, scalar=qkw_sb[:, 0:1], in1=q_hi[:, :].bitcast(F32),
                                                       op0=ALU.mult, op1=ALU.subtract).then_inc(qk_lo_ready, 1)
                    else:
                        dve.wait_ge(qk_turned, TWO(g, u, 1))
                        nc.vector.tensor_scalar(q_full[:, :], q_ps, qkw_sb[:, 0:1], None, ALU.mult).then_inc(qk_lo_ready, 1)
                    dve.wait_ge(qk_hi_ready, QK_PARTS(g, u, 2 if ui > 0 else 1))
                    if ui == 0:
                        nc.vector.tensor_scalar(k_full[:, :], k_ps, qkw_sb[:, 1:2], None, ALU.mult)
                    nc.vector.scalar_tensor_tensor(out=k_lo[:, b, ks], in0=k_ps, scalar=qkw_sb[:, 1:2], in1=k_hi[:, b, ks].bitcast(F32),
                                                   op0=ALU.mult, op1=ALU.subtract).then_inc(qk_lo_ready, 1)
                if here(t - 1, left):
                    dve.wait_ge(o_hi_ready, ONE(g, t - 1, 1))
                    nc.vector.tensor_tensor(o_lo[:, :], mix_ps[:, :], o_hi[:, :].bitcast(F32), ALU.subtract).then_inc(o_lo_ready, 1)
                if here(t - 2, left):
                    add_out(g, t - 2, left)

                def turned_lo(j):
                    dve.wait_ge(pt_hi_ready, PER_KEY_BLOCK(g, t, j + 1))
                    nc.vector.tensor_tensor(pt_lo[:, j, :], turn_ps[:, turn_slot(t, 2 + j), :], pt_hi[:, j, :].bitcast(F32),
                                            ALU.subtract).then_inc(pt_lo_ready, 1)

                if here(t + 2, left):
                    u, b, ui = t + 2, (t + 2) // QB % BATCH, (t + 2) % QB
                    if u % BLOCKS == 0:
                        if u > 0:
                            dve.wait_ge(inv_ready, ONE(g, u, 0))
                        col = (g + u // BLOCKS) * NORMED
                        nc.vector.tensor_copy(factor[:, :], cst[:, bass.ds(col + C_FACTOR, NORMED)]).then_inc(factor_set, 1)
                    dve.wait_ge(squares_ready, ONE(g, u, 1))
                    nc.vector.tensor_reduce(sums[:, :], squares[:, :, :], AX.X, ALU.add).then_inc(sums_ready, 1)
                    dve.wait_ge(sums_ready, ONE(g, u, 1))
                    nc.vector.tensor_scalar(mean_sq[:, :], sums[:, :], 1.0 / HD, RMS_EPS, ALU.mult, ALU.add).then_inc(mean_sq_ready, 1)
                if here(t, left):
                    for j in range(min(2, i + 1)):
                        turned_lo(j)
                if here(t + 2, left):
                    dve.wait_ge(v_hi_ready, ONE(g, u, 1))
                    nc.vector.tensor_tensor(v_lo[:, b, ui, :], v_ps, v_hi[:, b, ui, :].bitcast(F32), ALU.subtract).then_inc(v_lo_ready, 1)
                    dve.wait_ge(inv_rms_ready, ONE(g, u, 1))
                    dve.wait_ge(factor_set, g + (u // BLOCKS + 1))
                    nc.vector.tensor_tensor(inv[:, :], inv_rms[:, :], factor[:, :], ALU.mult).then_inc(inv_ready, 1)
                    dve.wait_ge(inv_ready, ONE(g, u, 1))
                    nc.vector.tensor_tensor(qk_norm[:, :, :], qkv_flat[:, 0:QK].rearrange("p (h d) -> p h d", h=NORMED),
                                            inv[:, :].unsqueeze(2).broadcast_to([P, NORMED, HD]), ALU.mult).then_inc(qk_norm_ready, 1)
                if here(t, left):
                    for j in range(2, i + 1):
                        turned_lo(j)

            def add_out(g, t, left):
                m = t % BLOCKS
                dve.wait_ge(out_ready, ONE(g, t, 1))
                nc.vector.tensor_tensor(acc[:, m, :], out_ps[:, :], acc[:, m, :], ALU.add).then_inc(acc_ready, 1)
                if left == 1:
                    if m == 0:
                        dve.wait_ge(gate_done, 2)
                        dve.wait_ge(x_again, 16)
                    dve.wait_ge(acc_ready, 1 + ONE(g, t, 1))
                    nc.vector.tensor_tensor(acc[:, m, :], acc[:, m, :], gate[:, m, :], ALU.mult).then_inc(gated_ready, 1)
                    dve.wait_ge(gated_ready, m + 1)
                    nc.vector.tensor_tensor(acc[:, m, :], acc[:, m, :], x_sb[:, m, :], ALU.add).then_inc(y_ready, 1)

            dve.wait_ge(acc_ready, 1)
            pipeline(dve, slot)

        @block.tensor
        def _(pe):
            def three(out, a_hi, a_lo, b_hi, b_lo, start, stop):
                pe.matmul(out, a_hi, b_hi, start=start, stop=False)
                pe.matmul(out, a_hi, b_lo, start=False, stop=False)
                return pe.matmul(out, a_lo, b_hi, start=False, stop=stop)

            def project(g, t):
                m = t % BLOCKS
                rows = slice(m * P, (m + 1) * P)
                if t > 0:
                    pe.wait_ge(qk_norm_ready, ONE(g, t - 1, 1))
                    pe.wait_ge(v_lo_ready, ONE(g, t - 1, 1))
                for c in range(KC):
                    if m == 0:
                        pe.wait_ge(w_lo_done, (g + t // BLOCKS) * KC + (c + 1))
                    for bank, lo, hi in ((0, 0, QW), (1, QW, QKV)):
                        last = three(qkv_ps[:, bank, 0:hi - lo], xt_hi[:, c, rows], xt_lo[:, c, rows],
                                     w_hi[:, c, lo:hi], w_lo[:, c, lo:hi], c == 0, c == KC - 1)
                last.then_inc(qkv_ready, 1)

            pe.wait_ge(small_loaded, 48)
            for t in range(BLOCKS):
                pe.wait_ge(xn_done, t + 1)
                if t >= 2:
                    pe.wait_ge(xt_lo_done, t - 1)
                for c in range(KC):
                    tr = pe.transpose(turn_ps[:, t % 2, c * P:(c + 1) * P], x_sb[:, t, c * P:(c + 1) * P], ident)
                tr.then_inc(xt_turned, 1)
            pe.wait_ge(ffn_lo_done, 2)
            pe.wait_ge(xt_lo_done, BLOCKS)
            for k in range(BLOCKS + 2):
                if k < BLOCKS:
                    if k >= 2:
                        pe.wait_ge(low_scaled, k - 1)
                    rows = slice(k * P, (k + 1) * P)
                    for c in range(KC):
                        last = three(score_ps[:, k % 2, 0:AW], xt_hi[:, c, rows], xt_lo[:, c, rows],
                                     aw_hi[:, c, :], aw_lo[:, c, :], c == 0, c == KC - 1)
                    last.then_inc(low_done, 1)
                if 1 <= k <= BLOCKS:
                    t = k - 1
                    pe.wait_ge(low_scaled, t + 1)
                    if t >= 2:
                        pe.wait_ge(lt_lo_done, t - 1)
                    pe.transpose(turn_ps[:, t % 2, 0:P], low[:, t % 2, :], ident).then_inc(low_turned, 1)
                if k >= 2:
                    t = k - 2
                    pe.wait_ge(lt_lo_done, t + 1)
                    if t >= 2:
                        pe.wait_ge(gate_in_kept, t - 1)
                    three(gate_ps[t % 2][:, :], lt_hi[:, t % 2, :], lt_lo[:, t % 2, :], bt_hi[:, :], bt_lo[:, :],
                          True, True).then_inc(gate_in_done, 1)
            pe.wait_ge(gate_in_kept, BLOCKS)

            def slot(g, t, left):
                n = keys_of(t) * P

                def scores(h):
                    if h == 0:
                        pe.wait_ge(qk_lo_ready, TWO(g, t, 2))
                    if t > 0 or h >= 2:
                        pe.wait_ge(biased_ready, PER_HEAD(g, t, h - 1))
                    hs, b = slice(h * HD, (h + 1) * HD), t // QB % BATCH
                    out = score_ps[:, h % 2, 0:n]
                    if t % QB == 0:
                        last = pe.matmul(out, q_full[:, hs], k_full[:, :], start=True, stop=True)
                    else:
                        last = three(out, q_hi[:, hs], q_lo[:, hs], k_hi[:, b, 0:n], k_lo[:, b, 0:n], True, True)
                    last.then_inc(scores_ready, 1)

                def turn_q():
                    pe.wait_ge(qk_norm_ready, ONE(g, t + 1, 1))
                    if t > 0:
                        if (t - 1) % QB == 0:
                            pe.wait_ge(qk_lo_ready, TWO(g, t, 2))
                        pe.wait_ge(pt_lo_ready, PER_KEY_BLOCK(g, t, 0))
                    for h in range(HPG):
                        tr = pe.transpose(turn_ps[:, turn_slot(t, 0), h * P:(h + 1) * P], qk_norm[:, h, :], ident)
                    tr.then_inc(qk_turned, 1)

                def turn_k():
                    pe.transpose(turn_ps[:, turn_slot(t, 1), 0:P], qk_norm[:, HPG, :], ident).then_inc(qk_turned, 1)

                def turn_probs(j):
                    if j >= 2:
                        pe.wait_ge(pt_lo_ready, PER_KEY_BLOCK(g, t, j - 1))
                    elif here(t + 1, left):
                        pe.wait_ge(qk_lo_ready, TWO(g, t + 1, j + 1))
                    else:
                        pe.wait_ge(pt_lo_ready, PER_KEY_BLOCK(g, t, 0))
                    if j == 0:
                        pe.wait_ge(probs_ready, PER_HEAD(g, t, HPG))
                    for h in range(HPG):
                        tr = pe.transpose(turn_ps[:, turn_slot(t, 2 + j), h * P:(h + 1) * P], probs[:, h, j * P:(j + 1) * P], ident)
                    tr.then_inc(probs_turned, 1)

                def mix(u, j):
                    i, b = u % QB, u // QB % BATCH
                    pe.wait_ge(pt_lo_ready, PER_KEY_BLOCK(g, u, j + 1))
                    if j == 0:
                        pe.wait_ge(v_lo_ready, ONE(g, u, 1))
                        if u > 0:
                            pe.wait_ge(o_lo_ready, ONE(g, u - 1, 1))
                    last = three(mix_ps[:, :], v_hi[:, b, j, :], v_lo[:, b, j, :], pt_hi[:, j, :], pt_lo[:, j, :], j == 0, j == i)
                    if j == i:
                        last.then_inc(mix_ready, 1)

                def out(u):
                    pe.wait_ge(o_lo_ready, ONE(g, u, 1))
                    pe.wait_ge(acc_ready, 1 + ONE(g, u - 1, 1))
                    for h in range(HPG):
                        if u % BLOCKS == 0:
                            pe.wait_ge(wo_lo_done, (g + u // BLOCKS) * HPG + (h + 1))
                        hs = slice(h * P, (h + 1) * P)
                        last = three(out_ps[:, :], o_hi[:, hs], o_lo[:, hs], wo_hi[:, h, :], wo_lo[:, h, :], h == 0, h == HPG - 1)
                    last.then_inc(out_ready, 1)

                i = t % QB
                if here(t, left):
                    scores(0)
                if here(t - 1, left):
                    mix(t - 1, (t - 1) % QB)
                if here(t, left):
                    scores(1)
                if here(t + 1, left):
                    turn_q()
                if here(t, left):
                    scores(2)
                if here(t + 1, left):
                    turn_k()
                if here(t, left):
                    scores(3)
                if here(t + 2, left):
                    project(g, t + 2)
                if here(t, left):
                    turn_probs(0)
                    if i >= 1:
                        turn_probs(1)
                if here(t - 1, left):
                    out(t - 1)
                if here(t, left):
                    for j in range(i):
                        mix(t, j)
                        if j + 2 <= i:
                            turn_probs(j + 2)
            pipeline(pe, slot)


def kernel(L0_attn_x, L0_attn_Wq, L0_attn_Wk, L0_attn_Wv, L0_attn_Wo, L0_attn_q_norm_w, L0_attn_k_norm_w,
           L0_ffn_A, L0_ffn_B, L0_ffn_Wr, L0_ffn_br):
    import concourse.bacc as bacc
    from concourse.bass_utils import run_bass_kernel_spmd

    def by_group(w, heads):
        return np.asarray(w).reshape(GROUPS, heads * HD, KC, P).transpose(0, 3, 2, 1)

    wqkv = np.concatenate([by_group(L0_attn_Wq, HPG), by_group(L0_attn_Wk, 1), by_group(L0_attn_Wv, 1)], axis=3)
    wo = np.asarray(L0_attn_Wo).reshape(DM, GROUPS, HPG, HD).transpose(1, 3, 2, 0)
    aw = np.concatenate([np.asarray(L0_ffn_A).reshape(LOW, DM), np.asarray(L0_ffn_Wr)], axis=0)
    aw = aw.reshape(LOW + EXPERTS, KC, P).transpose(2, 1, 0)
    arrays = {
        "x": np.asarray(L0_attn_x).reshape(BLOCKS * P, DM),
        "wqkv": wqkv.reshape(GROUPS, P, KC * QKV),
        "wo": wo.reshape(GROUPS, P, HPG * DM),
        "aw": aw.reshape(P, KC * (LOW + EXPERTS)),
        "bt": np.asarray(L0_ffn_B).transpose(0, 2, 1).reshape(LOW, DM),
        "br": np.broadcast_to(np.asarray(L0_ffn_br), (P, EXPERTS)),
        "qkw": np.stack([np.asarray(L0_attn_q_norm_w), np.asarray(L0_attn_k_norm_w)], axis=1),
        "consts": constants(),
    }
    arrays = {name: np.ascontiguousarray(a) for name, a in arrays.items()}
    nc = bacc.Bacc("TRN2", target_bir_lowering=False, num_devices=1)
    args = [nc.dram_tensor(name, a.shape, mybir.dt.from_np(a.dtype), kind="ExternalInput").ap() for name, a in arrays.items()]
    y = nc.dram_tensor("y", (BLOCKS * P, DM), F32, kind="ExternalOutput").ap()
    build(nc, *args, y)
    r = run_bass_kernel_spmd(nc, [arrays], core_ids=[0])
    return r.results[0]["y"].reshape(BATCH, SEQ, DM)
```

```python
from contextlib import ExitStack

import numpy as np

import concourse.bass as bass
from concourse import mybir

F32 = mybir.dt.float32
F32R = mybir.dt.float32r
ALU = mybir.AluOpType
ACT = mybir.ActivationFunctionType
AX = mybir.AxisListType

P = 128
BATCH, SEQ, DM = 2, 512, 512
HEADS, GROUPS, HD = 32, 8, 128
HPG = HEADS // GROUPS
QB = SEQ // P
BLOCKS = BATCH * QB
UNITS = GROUPS * BLOCKS
KC = DM // P
QW = HPG * HD
NORMED = HPG + 1
QK = NORMED * HD
QKV = QK + HD
EXPERTS, RANK = 8, 16
LOW = EXPERTS * RANK
AW = 256
FFN_SCALE = 2.0 * EXPERTS
LN_EPS, RMS_EPS = 1e-5, 1e-6
MASKED = 1e30
HUGE = 3e38
WARMING = 21

OUT_EARLY = {4: 1, 6: 3, 7: 5}
OUT_LATE = {5: 2, 6: 4}
OUT_LAST = 6
ADDS = {2: (0,), 5: (1,), 6: (2,), 7: (3, 4)}
ADDS_AT_END = {7: (5,)}
SILU_SLOT = 3
REST_SLOT = 5

C_IDENT = 0
C_DIST = C_IDENT + P
C_SLOPE = C_DIST + SEQ
C_FACTOR = C_SLOPE + HEADS
C_END = C_FACTOR + GROUPS * NORMED


def constants():
    import math
    start = 2 ** (-2 ** (-(math.log2(HEADS) - 3)))
    slopes = np.array([start * start ** i for i in range(HEADS)], dtype=np.float32)
    c = np.zeros((P, C_END), np.float32)
    c[:, C_IDENT:C_DIST] = np.eye(P)
    d = np.arange(P)[:, None] + (SEQ - P) - np.arange(SEQ)[None, :]
    c[:, C_DIST:C_SLOPE] = np.where(d < 0, MASKED, d)
    c[:, C_SLOPE:C_FACTOR] = slopes
    f = np.ones((GROUPS, NORMED))
    f[:, :HPG] = -1.0 / (slopes.astype(np.float64).reshape(GROUPS, HPG) * math.sqrt(HD))
    c[:, C_FACTOR:] = f.reshape(1, -1)
    return c


def counter(per_unit):
    n = len(per_unit)

    def value(g, t, e):
        return g * sum(per_unit) + (t // n) * sum(per_unit) + sum(per_unit[:t % n]) + e
    return value


ONE = counter([1] * BLOCKS)
TWO = counter([2] * BLOCKS)
PER_HEAD = counter([HPG] * BLOCKS)
PER_KEY_BLOCK = counter([i + 1 for i in range(QB)] * BATCH)
PER_BATCH = counter(([1] + [0] * (QB - 1)) * BATCH)
K_AND_Q_LO = counter(([1] + [2] * (QB - 1)) * BATCH)


def keys_of(t):
    return t % QB + 1


def build(nc, x, wqkv, wo, aw, bt, br, qkw, consts, y):
    with ExitStack() as ctx:
        def sb(name, shape, dt=F32):
            return ctx.enter_context(nc.sbuf_tensor(name, [P, *shape], dt))

        def psum(name, shape):
            return ctx.enter_context(nc.psum_tensor(name, [P, *shape], F32))

        def sem(name):
            return ctx.enter_context(nc.semaphore(name))

        cst = sb("cst", [C_END])
        ident = cst[:, C_IDENT:C_DIST]
        qkw_sb = sb("qkw_sb", [2])
        br_sb = sb("br_sb", [EXPERTS])
        x_sb = sb("x_sb", [BLOCKS, DM])
        xt_hi, xt_lo = (sb(f"xt_{p}", [KC, BLOCKS * P], F32R) for p in ("hi", "lo"))
        w_raw = sb("w_raw", [KC, QKV])
        w_hi, w_lo = (sb(f"w_{p}", [KC, QKV], F32R) for p in ("hi", "lo"))
        wo_raw = sb("wo_raw", [HPG, DM])
        wo_hi, wo_lo = (sb(f"wo_{p}", [HPG, DM], F32R) for p in ("hi", "lo"))
        bt_hi, bt_lo = (sb(f"bt_{p}", [DM], F32R) for p in ("hi", "lo"))
        squares = sb("squares", [NORMED, HD])
        qk_norm = sb("qk_norm", [NORMED, HD])
        q_full = sb("q_full", [QW])
        k_full = sb("k_full", [P])
        q_hi, q_lo = (sb(f"q_{p}", [QW], F32R) for p in ("hi", "lo"))
        k_hi, k_lo = (sb(f"k_{p}", [BATCH, SEQ], F32R) for p in ("hi", "lo"))
        v_hi, v_lo = (sb(f"v_{p}", [BATCH, QB, HD], F32R) for p in ("hi", "lo"))
        probs = sb("probs", [HPG, SEQ])
        pt_hi, pt_lo = (sb(f"pt_{p}", [QB, HPG * P], F32R) for p in ("hi", "lo"))
        o_hi, o_lo = (sb(f"o_{p}", [HPG, P], F32R) for p in ("hi", "lo"))
        acc = sb("acc", [BLOCKS, DM])
        gate = sb("gate", [BLOCKS, DM])
        slope = sb("slope", [HPG])
        factor = sb("factor", [NORMED])
        sums = sb("sums", [NORMED])
        mean_sq = sb("mean_sq", [NORMED])
        inv_rms = sb("inv_rms", [NORMED])
        inv = sb("inv", [NORMED])
        minus_half = sb("minus_half", [8])
        neg_max = sb("neg_max", [HPG])
        total = sb("total", [HPG])
        recip = sb("recip", [HPG])
        bn = sb("bn", [BLOCKS, 6])
        moments = sb("moments", [BLOCKS, 2])
        var_eps = sb("var_eps", [BLOCKS])
        rstd = sb("rstd", [BLOCKS])
        logits = sb("logits", [2, EXPERTS])
        logit_max = sb("logit_max", [2])
        route = sb("route", [2, EXPERTS])
        route_sum = sb("route_sum", [2])
        route_inv = sb("route_inv", [2])
        low = probs[:, 0:2, 2 * P:4 * P].rearrange("p a (s l) -> p a s l", s=2)
        aw_raw = sb("aw_raw", [KC, LOW + EXPERTS])
        aw_hi = wo_hi[:, 2:HPG, :].rearrange("p a (b n) -> p (a b) n", b=2)
        aw_lo = wo_lo[:, 2:HPG, :].rearrange("p a (b n) -> p (a b) n", b=2)
        lt_hi = pt_hi[:, 2, :].rearrange("p (a s n) -> p a s n", a=2, s=2)
        lt_lo = pt_lo[:, 2, :].rearrange("p (a s n) -> p a s n", a=2, s=2)
        bt_raw = gate[:, BLOCKS - 1, :]

        qkv_ps = psum("qkv_ps", [2, 512])
        score_ps = psum("score_ps", [2, 512])
        turn_ps = psum("turn_ps", [2, 512])
        mix_ps = psum("mix_ps", [512])
        mixed = mix_ps[:, :].rearrange("p (h n) -> p h n", h=HPG)
        out_ps = psum("out_ps", [512])
        qkv_flat = qkv_ps[:, :, :].rearrange("p a n -> p (a n)")
        v_ps = qkv_flat[:, QK:QKV]
        last_out_ps = {3: qkv_ps[:, 0, :], 4: qkv_ps[:, 1, :], 6: qkv_ps[:, 0, :]}
        halves = [slice(0, DM // 2), slice(DM // 2, DM)]
        ffn_ps = [mix_ps, out_ps]
        gate_ps = [ffn_ps[b] for b in (0, 1, 0, 1, 0, 1, 1, 0)]
        low_ps = [b[:, :].rearrange("p (s n) -> p s n", s=2) for b in ffn_ps]
        lt_ps = [score_ps[:, b, 0:2 * P].rearrange("p (s n) -> p s n", s=2) for b in (0, 0, 0, 1)]

        x_loaded = [sem(f"x_loaded{t}") for t in range(BLOCKS)]
        ident_loaded = sem("ident_loaded")
        small_loaded = sem("small_loaded")
        ffn_loaded = sem("ffn_loaded")
        bt_loaded = sem("bt_loaded")
        w_first = [sem(f"w_first{c}") for c in range(KC)]
        w_loaded = sem("w_loaded")
        wo_loaded = sem("wo_loaded")
        x_again = sem("x_again")
        stored = sem("stored")
        half_set = sem("half_set")
        bn_done = sem("bn_done")
        moments_done = sem("moments_done")
        var_done = sem("var_done")
        rstd_done = sem("rstd_done")
        xn_done = sem("xn_done")
        xt_turned = sem("xt_turned")
        xt_hi_done = sem("xt_hi_done")
        xt_lo_done = sem("xt_lo_done")
        aw_zeroed = sem("aw_zeroed")
        ffn_hi_done = sem("ffn_hi_done")
        ffn_lo_done = sem("ffn_lo_done")
        low_done = sem("low_done")
        logits_done = sem("logits_done")
        route_done = sem("route_done")
        route_inv_done = sem("route_inv_done")
        low_scaled = sem("low_scaled")
        low_turned = sem("low_turned")
        lt_hi_done = sem("lt_hi_done")
        lt_lo_done = sem("lt_lo_done")
        gate_in_done = sem("gate_in_done")
        gate_in_kept = sem("gate_in_kept")
        gate_done = sem("gate_done")
        w_hi_done = sem("w_hi_done")
        w_lo_done = sem("w_lo_done")
        wo_hi_done = sem("wo_hi_done")
        wo_lo_done = sem("wo_lo_done")
        slope_set = sem("slope_set")
        factor_set = sem("factor_set")
        qkv_ready = sem("qkv_ready")
        squares_ready = sem("squares_ready")
        sums_ready = sem("sums_ready")
        mean_sq_ready = sem("mean_sq_ready")
        inv_rms_ready = sem("inv_rms_ready")
        inv_ready = sem("inv_ready")
        qk_norm_ready = sem("qk_norm_ready")
        v_hi_ready = sem("v_hi_ready")
        v_lo_ready = sem("v_lo_ready")
        qk_turned = sem("qk_turned")
        qk_hi_ready = sem("qk_hi_ready")
        k_full_ready = sem("k_full_ready")
        qk_lo_ready = sem("qk_lo_ready")
        scores_ready = sem("scores_ready")
        scores_taken = sem("scores_taken")
        biased_ready = sem("biased_ready")
        exp_ready = sem("exp_ready")
        recip_ready = sem("recip_ready")
        probs_ready = sem("probs_ready")
        probs_turned = sem("probs_turned")
        pt_hi_ready = sem("pt_hi_ready")
        pt_lo_ready = sem("pt_lo_ready")
        mix_ready = sem("mix_ready")
        o_hi_ready = sem("o_hi_ready")
        o_lo_ready = sem("o_lo_ready")
        out_ready = sem("out_ready")
        acc_ready = sem("acc_ready")
        gated_ready = sem("gated_ready")
        y_ready = sem("y_ready")
        rest_gated = sem("rest_gated")
        rest_ready = sem("rest_ready")
        share_gated = sem("share_gated")
        last_y_ready = sem("last_y_ready")

        def turn_slot(s, n):
            per = [keys_of(i) + 2 for i in range(QB)]
            return (sum(per) * (s // QB) + sum(per[:s % QB]) + n) % 2

        def pipeline(eng, slot):
            with eng.Fori(0, GROUPS - 1) as g:
                for t in range(2, BLOCKS + 2):
                    slot(g, t, GROUPS)
            for t in range(2, BLOCKS + 2):
                slot(GROUPS - 1, t, 1)

        def held_back(t, left):
            return left == 1 and t not in OUT_LATE and t not in OUT_EARLY and here(t + 2, left)

        def o_parts(u, left):
            if left == 1:
                rows = slice(u % BLOCKS * P, (u % BLOCKS + 1) * P)
                return xt_hi[:, :, rows], xt_lo[:, :, rows]
            return o_hi[:, :, :], o_lo[:, :, :]

        def out_bank(u, left):
            return last_out_ps.get(u, out_ps[:, :]) if left == 1 else out_ps[:, :]

        def here(t, left):
            return 0 <= t < BLOCKS * left

        block = ctx.enter_context(nc.Block())

        @block.sync
        def _(sp):
            def load_x(t):
                sp.dma_start(x_sb[:, t, :], x[t * P:(t + 1) * P, :]).then_inc(x_loaded[t], 16)

            def load_w(c):
                sp.dma_start(w_raw[:, c, :], wqkv[0:1, :, c * QKV:(c + 1) * QKV].rearrange("a p n -> p (a n)")).then_inc(w_first[c], 16)

            load_x(0)
            load_w(0)
            sp.dma_start(ident, consts[:, C_IDENT:C_DIST]).then_inc(ident_loaded, 16)
            load_x(1)
            for c in range(1, KC):
                load_w(c)
            load_x(2)
            sp.dma_start(aw_raw[:, :, :].rearrange("p c n -> p (c n)"), aw).then_inc(ffn_loaded, 16)
            sp.dma_start(cst[:, C_DIST:C_END], consts[:, C_DIST:C_END]).then_inc(small_loaded, 16)
            sp.dma_start(br_sb[:, :], br).then_inc(small_loaded, 16)
            sp.dma_start(qkw_sb[:, :], qkw).then_inc(small_loaded, 16)
            for t in range(3, 6):
                load_x(t)
            sp.dma_start(bt_raw, bt).then_inc(bt_loaded, 16)
            for t in range(6, BLOCKS):
                load_x(t)
            sp.dma_start(wo_raw[:, :, :].rearrange("p c n -> p (c n)"), wo[0:1].rearrange("a p n -> p (a n)")).then_inc(wo_loaded, 16)
            sp.wait_ge(xt_turned, BLOCKS)
            sp.dma_start(x_sb[:, :, :], x.rearrange("(t p) n -> p t n", p=P)).then_inc(x_again, 16)
            with sp.Fori(0, GROUPS - 1) as g:
                sp.wait_ge(w_lo_done, g * KC + KC)
                sp.dma_start(w_raw[:, :, :].rearrange("p c n -> p (c n)"), wqkv[bass.ds(g + 1, 1)].rearrange("a p n -> p (a n)")).then_inc(w_loaded, 16)
                sp.wait_ge(wo_lo_done, g * HPG + HPG)
                sp.dma_start(wo_raw[:, :, :].rearrange("p c n -> p (c n)"), wo[bass.ds(g + 1, 1)].rearrange("a p n -> p (a n)")).then_inc(wo_loaded, 16)
            for t in range(BLOCKS - 2):
                sp.wait_ge(y_ready, t + 1)
                sp.dma_start(y[t * P:(t + 1) * P, :], acc[:, t, :]).then_inc(stored, 16)
            sp.wait_ge(last_y_ready, 1)
            sp.dma_start(y[(BLOCKS - 2) * P:(BLOCKS - 1) * P, :], acc[:, BLOCKS - 2, :]).then_inc(stored, 16)
            for k, cols in enumerate(halves):
                sp.wait_ge(last_y_ready, k + 2)
                sp.dma_start(y[(BLOCKS - 1) * P:BLOCKS * P, cols], acc[:, BLOCKS - 1, cols]).then_inc(stored, 16)
            sp.wait_ge(stored, 16 * (BLOCKS + 1))

        @block.gpsimd
        def _(pool):
            nc.gpsimd.memset(minus_half[:, :], -0.5).then_inc(half_set, 1)
            nc.gpsimd.memset(acc[:, :, :], 0.0).then_inc(acc_ready, 1)
            pool.wait_ge(half_set, 1)

            def inverse_std(t):
                pool.wait_ge(var_done, t + 1)
                nc.gpsimd.tensor_tensor(rstd[:, t:t + 1], var_eps[:, t:t + 1], minus_half[:, 0:1], ALU.pow).then_inc(rstd_done, 1)

            def split_w(group, chunks=range(KC)):
                for c in chunks:
                    pool.wait_ge(w_hi_done, group * KC + (c + 1))
                    nc.gpsimd.tensor_tensor(w_lo[:, c, :], w_raw[:, c, :], w_hi[:, c, :].bitcast(F32),
                                            ALU.subtract).then_inc(w_lo_done, 1)

            def split_wo(group, heads):
                for h in heads:
                    pool.wait_ge(wo_hi_done, group * HPG + (h + 1))
                    nc.gpsimd.tensor_tensor(wo_lo[:, h, :], wo_raw[:, h, :], wo_hi[:, h, :].bitcast(F32),
                                            ALU.subtract).then_inc(wo_lo_done, 1)

            def inverse_rms(g, u):
                pool.wait_ge(mean_sq_ready, ONE(g, u, 1))
                nc.gpsimd.tensor_tensor(inv_rms[:, :], mean_sq[:, :], minus_half[:, 0:NORMED],
                                        ALU.pow).then_inc(inv_rms_ready, 1)

            def finish_y(m):
                if m == 0:
                    pool.wait_ge(x_again, 16)
                pool.wait_ge(gate_done, 1)
                pool.wait_ge(acc_ready, 1 + ONE(GROUPS - 1, m, 1))
                nc.gpsimd.tensor_tensor(acc[:, m, :], acc[:, m, :], gate[:, m, :], ALU.mult).then_inc(gated_ready, 1)
                pool.wait_ge(gated_ready, m + 1)
                nc.gpsimd.tensor_tensor(acc[:, m, :], acc[:, m, :], x_sb[:, m, :], ALU.add).then_inc(y_ready, 1)

            def start_last_y():
                pool.wait_ge(gate_done, 1)
                for k, m in enumerate((BLOCKS - 2, BLOCKS - 1)):
                    nc.gpsimd.tensor_tensor(acc[:, m, :], acc[:, m, :], gate[:, m, :], ALU.mult).then_inc(rest_gated, 1)
                    pool.wait_ge(rest_gated, k + 1)
                    nc.gpsimd.tensor_tensor(x_sb[:, m, :], x_sb[:, m, :], acc[:, m, :], ALU.add).then_inc(rest_ready, 1)

            def slot(g, t, left):
                if t % BLOCKS == 1 and here(t, left):
                    split_wo(g + t // BLOCKS, range(2, HPG))
                if here(t + 2, left):
                    inverse_rms(g, t + 2)
                if t % BLOCKS == BLOCKS - 3 and here(t + 3, left):
                    split_w(g + 1)
                if t % BLOCKS == 0 and here(t, left):
                    split_wo(g + t // BLOCKS, range(0, 2))
                if left == 1:
                    if t == REST_SLOT:
                        start_last_y()
                    for s in range(2 if t == SILU_SLOT + 1 else t, t + 1):
                        for m in ADDS.get(s, ()) + ADDS_AT_END.get(s, ()):
                            if t > SILU_SLOT:
                                finish_y(m)

            inverse_std(0)
            split_w(0, range(1))
            inverse_std(1)
            inverse_std(2)
            inverse_rms(0, 0)
            for t in range(3, 6):
                inverse_std(t)
            inverse_rms(0, 1)
            for t in range(6, BLOCKS):
                inverse_std(t)
            split_wo(0, range(0, 2))
            inverse_rms(0, 2)
            inverse_rms(0, 3)
            split_wo(0, range(2, HPG))
            pipeline(pool, slot)

        @block.scalar
        def _(act):
            def split_w(group):
                act.wait_ge(w_loaded, group * 16)
                for c in range(KC):
                    nc.scalar.activation(w_hi[:, c, :], w_raw[:, c, :], ACT.Copy).then_inc(w_hi_done, 1)

            def split_first_w(chunks):
                for c in chunks:
                    act.wait_ge(w_first[c], 16)
                    nc.scalar.activation(w_hi[:, c, :], w_raw[:, c, :], ACT.Copy).then_inc(w_hi_done, 1)

            def split_wo(group, heads):
                act.wait_ge(wo_loaded, group * 16 + 16)
                for h in heads:
                    nc.scalar.activation(wo_hi[:, h, :], wo_raw[:, h, :], ACT.Copy).then_inc(wo_hi_done, 1)

            def turned_x_hi(t):
                act.wait_ge(xt_turned, t + 1)
                nc.scalar.activation(xt_hi[:, :, t * P:(t + 1) * P],
                                     turn_ps[:, t % 2, :].rearrange("p (c n) -> p c n", c=KC),
                                     ACT.Copy).then_inc(xt_hi_done, 1)

            def route_exp(p):
                act.wait_ge(logits_done, 2 * p + 2)
                for b in range(2):
                    nc.scalar.activation(route[:, b, :], logits[:, b, :], ACT.Exp, bias=logit_max[:, b:b + 1], scale=-1.0,
                                         accum_out=route_sum[:, b:b + 1]).then_inc(route_done, 1)

            def turned_low_hi(p):
                act.wait_ge(low_turned, p + 1)
                nc.scalar.activation(lt_hi[:, p % 2, :, :], lt_ps[p], ACT.Copy).then_inc(lt_hi_done, 1)

            def keep_gate_in(t):
                act.wait_ge(gate_in_done, t + 1)
                nc.scalar.activation(gate[:, t, :], gate_ps[t][:, :], ACT.Copy, scale=FFN_SCALE).then_inc(gate_in_kept, 1)

            def gates():
                nc.scalar.activation(gate[:, :, :], gate[:, :, :], ACT.Silu).then_inc(gate_done, 1)

            def exponentials(g, t, heads):
                n = keys_of(t) * P
                for h in heads:
                    act.wait_ge(biased_ready, PER_HEAD(g, t, h + 1))
                    nc.scalar.activation(probs[:, h, 0:n], probs[:, h, 0:n], ACT.Exp, bias=neg_max[:, h:h + 1],
                                         scale=-1.0, accum_out=total[:, h:h + 1]).then_inc(exp_ready, 1)

            def mixed_hi(g, u, left):
                act.wait_ge(mix_ready, ONE(g, u, 1))
                nc.scalar.activation(o_parts(u, left)[0], mixed, ACT.Copy).then_inc(o_hi_ready, 1)

            def turned_qk_hi(g, u):
                t, b, ui = u - 1, u // QB % BATCH, u % QB
                q_ps, k_ps = turn_ps[:, turn_slot(t, 0), :], turn_ps[:, turn_slot(t, 1), 0:P]
                act.wait_ge(qk_turned, TWO(g, u, 1))
                nc.scalar.activation(q_hi[:, :] if ui > 0 else q_full[:, :], q_ps, ACT.Copy, scale=qkw_sb[:, 0:1]).then_inc(qk_hi_ready, 1)
                act.wait_ge(qk_turned, TWO(g, u, 2))
                if ui == 0:
                    nc.scalar.activation(k_full[:, :], k_ps, ACT.Copy, scale=qkw_sb[:, 1:2]).then_inc(k_full_ready, 1)
                nc.scalar.activation(k_hi[:, b, ui * P:(ui + 1) * P], k_ps, ACT.Copy, scale=qkw_sb[:, 1:2]).then_inc(qk_hi_ready, 1)

            def square_qk(g, u):
                act.wait_ge(qkv_ready, ONE(g, u, 1))
                nc.scalar.activation(squares[:, :, :].rearrange("p h d -> p (h d)"), qkv_flat[:, 0:QK],
                                     ACT.Square).then_inc(squares_ready, 1)

            def value_hi(g, u):
                nc.scalar.activation(v_hi[:, u // QB % BATCH, u % QB, :], v_ps, ACT.Copy).then_inc(v_hi_ready, 1)

            def turned_hi(g, t, j):
                act.wait_ge(probs_turned, PER_KEY_BLOCK(g, t, j + 1))
                nc.scalar.activation(pt_hi[:, j, :], turn_ps[:, turn_slot(t, 2 + j), :], ACT.Copy).then_inc(pt_hi_ready, 1)

            def slot(g, t, left):
                i = t % QB
                if here(t, left):
                    exponentials(g, t, range(0, 2))
                if here(t - 1, left):
                    mixed_hi(g, t - 1, left)
                if here(t, left):
                    exponentials(g, t, range(2, HPG))
                if here(t + 1, left):
                    turned_qk_hi(g, t + 1)
                split = held_back(t, left)
                if t % BLOCKS == 1 and here(t, left):
                    split_wo(g + t // BLOCKS, range(2, HPG))
                if here(t + 2, left) and not split:
                    square_qk(g, t + 2)
                if here(t, left):
                    for j in range(min(2, i + 1)):
                        turned_hi(g, t, j)
                if here(t + 2, left):
                    if split:
                        square_qk(g, t + 2)
                        turned_hi(g, t, 2)
                    value_hi(g, t + 2)
                if here(t, left):
                    for j in range(3 if split else 2, i + 1):
                        turned_hi(g, t, j)
                if t % BLOCKS == BLOCKS - 3 and here(t + 3, left):
                    split_w(g + 1)
                if t % BLOCKS == 0 and here(t, left):
                    act.wait_ge(out_ready, ONE(g, t - 1, 1))
                    split_wo(g + t // BLOCKS, range(0, 2))
                if left == 1 and t == SILU_SLOT:
                    gates()

            split_first_w(range(0, 1))
            turned_x_hi(0)
            split_first_w(range(1, KC))
            turned_x_hi(1)
            act.wait_ge(ffn_loaded, 16)
            act.wait_ge(aw_zeroed, 3)
            nc.scalar.activation(aw_hi[:, :, 0:LOW + EXPERTS], aw_raw[:, :, :], ACT.Copy).then_inc(ffn_hi_done, 1)
            square_qk(0, 0)
            value_hi(0, 0)
            act.wait_ge(bt_loaded, 16)
            nc.scalar.activation(bt_hi[:, :], bt_raw, ACT.Copy).then_inc(ffn_hi_done, 1)
            route_exp(0)
            turned_x_hi(2)
            turned_x_hi(3)
            square_qk(0, 1)
            value_hi(0, 1)
            turned_low_hi(0)
            act.wait_ge(small_loaded, 48)
            turned_qk_hi(0, 0)
            turned_x_hi(4)
            turned_x_hi(5)
            route_exp(1)
            exponentials(0, 0, range(0, 2))
            keep_gate_in(0)
            exponentials(0, 0, range(2, HPG))
            turned_qk_hi(0, 1)
            turned_low_hi(1)
            split_wo(0, range(0, 2))
            square_qk(0, 2)
            value_hi(0, 2)
            keep_gate_in(1)
            turned_x_hi(6)
            turned_x_hi(7)
            keep_gate_in(2)
            keep_gate_in(3)
            route_exp(2)
            turned_hi(0, 0, 0)
            exponentials(0, 1, range(0, 2))
            route_exp(3)
            exponentials(0, 1, range(2, HPG))
            turned_qk_hi(0, 2)
            turned_low_hi(2)
            split_wo(0, range(2, HPG))
            square_qk(0, 3)
            value_hi(0, 3)
            keep_gate_in(4)
            turned_low_hi(3)
            keep_gate_in(5)
            mixed_hi(0, 0, GROUPS)
            for j in range(2):
                turned_hi(0, 1, j)
            keep_gate_in(6)
            keep_gate_in(7)
            pipeline(act, slot)

        @block.vector
        def _(dve):
            nc.vector.memset(aw_hi[:, 0, :].bitcast(F32), 0.0).then_inc(aw_zeroed, 1)
            nc.vector.memset(aw_hi[:, 1:KC, :].bitcast(F32), 0.0).then_inc(aw_zeroed, 1)
            nc.vector.memset(aw_lo.bitcast(F32), 0.0).then_inc(aw_zeroed, 1)

            def moments_of(t):
                dve.wait_ge(x_loaded[t], 16)
                nc.vector.bn_stats(bn[:, t, :], x_sb[:, t, :]).then_inc(bn_done, 1)
                dve.wait_ge(bn_done, t + 1)
                nc.vector.bn_aggr(moments[:, t, :], bn[:, t, :]).then_inc(moments_done, 1)
                dve.wait_ge(moments_done, t + 1)
                nc.vector.tensor_scalar(var_eps[:, t:t + 1], moments[:, t, 1:2], LN_EPS, None, ALU.add).then_inc(var_done, 1)

            def normalize_x(t):
                dve.wait_ge(rstd_done, t + 1)
                nc.vector.tensor_scalar(x_sb[:, t, :], x_sb[:, t, :], moments[:, t, 0:1], rstd[:, t:t + 1],
                                        ALU.subtract, ALU.mult).then_inc(xn_done, 1)

            def split_first_w(c):
                dve.wait_ge(w_hi_done, c + 1)
                dve.wait_ge(w_lo_done, c)
                nc.vector.tensor_tensor(w_lo[:, c, :], w_raw[:, c, :], w_hi[:, c, :].bitcast(F32),
                                        ALU.subtract).then_inc(w_lo_done, 1)

            def turned_x_lo(t):
                dve.wait_ge(xt_hi_done, t + 1)
                nc.vector.tensor_tensor(xt_lo[:, :, t * P:(t + 1) * P],
                                        turn_ps[:, t % 2, :].rearrange("p (c n) -> p c n", c=KC),
                                        xt_hi[:, :, t * P:(t + 1) * P].bitcast(F32), ALU.subtract).then_inc(xt_lo_done, 1)

            def router_logits(p):
                dve.wait_ge(low_done, p + 1)
                for b in range(2):
                    nc.vector.tensor_tensor_reduce(logits[:, b, :], low_ps[p % 2][:, b, LOW:LOW + EXPERTS], br_sb[:, :],
                                                   -1.0, HUGE, ALU.add, ALU.min, logit_max[:, b:b + 1]).then_inc(logits_done, 1)

            def scale_low(p):
                dve.wait_ge(route_done, 2 * p + 2)
                nc.vector.reciprocal(route_inv[:, :], route_sum[:, :]).then_inc(route_inv_done, 1)
                dve.wait_ge(route_inv_done, p + 1)
                for b in range(2):
                    nc.vector.scalar_tensor_tensor(
                        out=low[:, p % 2, b, :].rearrange("p (e r) -> p e r", e=EXPERTS),
                        in0=low_ps[p % 2][:, b, 0:LOW].rearrange("p (e r) -> p e r", e=EXPERTS), scalar=route_inv[:, b:b + 1],
                        in1=route[:, b, :].unsqueeze(2).broadcast_to([P, EXPERTS, RANK]),
                        op0=ALU.mult, op1=ALU.mult).then_inc(low_scaled, 1)

            def turned_low_lo(p):
                dve.wait_ge(lt_hi_done, p + 1)
                nc.vector.tensor_tensor(lt_lo[:, p % 2, :, :], lt_ps[p], lt_hi[:, p % 2, :, :].bitcast(F32),
                                        ALU.subtract).then_inc(lt_lo_done, 1)

            def set_slope(g, t):
                if t > 0:
                    dve.wait_ge(biased_ready, PER_HEAD(g, t, 0))
                col = (g + t // BLOCKS) * HPG
                nc.vector.tensor_copy(slope[:, :], cst[:, bass.ds(col + C_SLOPE, HPG)]).then_inc(slope_set, 1)
                dve.wait_ge(slope_set, g + (t // BLOCKS + 1))

            def set_factor(g, u):
                if u > 0:
                    dve.wait_ge(inv_ready, ONE(g, u, 0))
                col = (g + u // BLOCKS) * NORMED
                nc.vector.tensor_copy(factor[:, :], cst[:, bass.ds(col + C_FACTOR, NORMED)]).then_inc(factor_set, 1)

            def bias(g, t, h):
                n = keys_of(t) * P
                dve.wait_ge(scores_ready, PER_HEAD(g, t, h + 1))
                dve.sem_inc(scores_taken, 1)
                nc.vector.tensor_tensor_reduce(
                    probs[:, h, 0:n], score_ps[:, h % 2, 0:n], cst[:, C_DIST + SEQ - n:C_DIST + SEQ],
                    slope[:, h:h + 1], HUGE, ALU.add, ALU.min, neg_max[:, h:h + 1]).then_inc(biased_ready, 1)

            def normalize_probs(g, t):
                n = keys_of(t) * P
                for h in range(0, HPG, 2):
                    dve.wait_ge(exp_ready, PER_HEAD(g, t, h + 2))
                    nc.vector.reciprocal(recip[:, h:h + 2], total[:, h:h + 2]).then_inc(recip_ready, 1)
                    dve.wait_ge(recip_ready, TWO(g, t, h // 2 + 1))
                    for hh in (h, h + 1):
                        nc.vector.tensor_scalar(probs[:, hh, 0:n], probs[:, hh, 0:n], recip[:, hh:hh + 1], None,
                                                ALU.mult).then_inc(probs_ready, 1)

            def turned_qk_lo(g, u):
                t, b, ui = u - 1, u // QB % BATCH, u % QB
                ks = slice(ui * P, (ui + 1) * P)
                q_ps, k_ps = turn_ps[:, turn_slot(t, 0), :], turn_ps[:, turn_slot(t, 1), 0:P]
                if ui > 0:
                    dve.wait_ge(qk_hi_ready, TWO(g, u, 1))
                    nc.vector.scalar_tensor_tensor(out=q_lo[:, :], in0=q_ps, scalar=qkw_sb[:, 0:1], in1=q_hi[:, :].bitcast(F32),
                                                   op0=ALU.mult, op1=ALU.subtract).then_inc(qk_lo_ready, 1)
                dve.wait_ge(qk_hi_ready, TWO(g, u, 2))
                nc.vector.scalar_tensor_tensor(out=k_lo[:, b, ks], in0=k_ps, scalar=qkw_sb[:, 1:2], in1=k_hi[:, b, ks].bitcast(F32),
                                               op0=ALU.mult, op1=ALU.subtract).then_inc(qk_lo_ready, 1)

            def mixed_lo(g, u, left):
                hi, lo = o_parts(u, left)
                dve.wait_ge(o_hi_ready, ONE(g, u, 1))
                nc.vector.tensor_tensor(lo, mixed, hi.bitcast(F32), ALU.subtract).then_inc(o_lo_ready, 1)

            def mean_square(g, u):
                dve.wait_ge(squares_ready, ONE(g, u, 1))
                nc.vector.tensor_reduce(sums[:, :], squares[:, :, :], AX.X, ALU.add).then_inc(sums_ready, 1)
                dve.wait_ge(sums_ready, ONE(g, u, 1))
                nc.vector.tensor_scalar(mean_sq[:, :], sums[:, :], 1.0 / HD, RMS_EPS, ALU.mult, ALU.add).then_inc(mean_sq_ready, 1)

            def value_lo(g, u):
                b, ui = u // QB % BATCH, u % QB
                dve.wait_ge(v_hi_ready, ONE(g, u, 1))
                nc.vector.tensor_tensor(v_lo[:, b, ui, :], v_ps, v_hi[:, b, ui, :].bitcast(F32), ALU.subtract).then_inc(v_lo_ready, 1)

            def normalize_qk(g, u):
                dve.wait_ge(inv_rms_ready, ONE(g, u, 1))
                dve.wait_ge(factor_set, g + (u // BLOCKS + 1))
                nc.vector.tensor_tensor(inv[:, :], inv_rms[:, :], factor[:, :], ALU.mult).then_inc(inv_ready, 1)
                dve.wait_ge(inv_ready, ONE(g, u, 1))
                nc.vector.tensor_tensor(qk_norm[:, :, :], qkv_flat[:, 0:QK].rearrange("p (h d) -> p h d", h=NORMED),
                                        inv[:, :].unsqueeze(2).broadcast_to([P, NORMED, HD]), ALU.mult).then_inc(qk_norm_ready, 1)

            def turned_lo(g, t, j):
                dve.wait_ge(pt_hi_ready, PER_KEY_BLOCK(g, t, j + 1))
                nc.vector.tensor_tensor(pt_lo[:, j, :], turn_ps[:, turn_slot(t, 2 + j), :], pt_hi[:, j, :].bitcast(F32),
                                        ALU.subtract).then_inc(pt_lo_ready, 1)

            def add_out(g, u, left):
                m = u % BLOCKS
                dve.wait_ge(out_ready, ONE(g, u, 1))
                nc.vector.tensor_tensor(acc[:, m, :], out_bank(u, left), acc[:, m, :], ALU.add).then_inc(acc_ready, 1)

            def last_y(m, k, share, cols):
                dve.wait_ge(rest_ready, m - (BLOCKS - 2) + 1)
                dve.wait_ge(out_ready, ONE(GROUPS - 1, BLOCKS - 2, k + 1))
                nc.vector.tensor_tensor(acc[:, m, cols], share, gate[:, m, cols], ALU.mult).then_inc(share_gated, 1)
                dve.wait_ge(share_gated, k + 1)
                nc.vector.tensor_tensor(acc[:, m, cols], acc[:, m, cols], x_sb[:, m, cols], ALU.add).then_inc(last_y_ready, 1)

            def slot(g, t, left):
                i = t % QB
                if t % BLOCKS == 0 and here(t, left):
                    set_slope(g, t)
                if here(t, left):
                    for h in range(HPG):
                        bias(g, t, h)
                    normalize_probs(g, t)
                if here(t + 1, left):
                    turned_qk_lo(g, t + 1)
                if here(t - 1, left):
                    mixed_lo(g, t - 1, left)
                for m in (t - 2,) if left > 1 else ADDS.get(t, ()):
                    add_out(g, m, left)
                split = held_back(t, left)
                if here(t + 2, left) and not split:
                    if (t + 2) % BLOCKS == 0:
                        set_factor(g, t + 2)
                    mean_square(g, t + 2)
                if here(t, left):
                    for j in range(min(2, i + 1)):
                        turned_lo(g, t, j)
                if here(t + 2, left):
                    if split:
                        mean_square(g, t + 2)
                        turned_lo(g, t, 2)
                    value_lo(g, t + 2)
                    if split and i == 3:
                        turned_lo(g, t, 3)
                    normalize_qk(g, t + 2)
                if here(t, left) and not split:
                    for j in range(2, i + 1):
                        turned_lo(g, t, j)
                if left == 1:
                    for m in ADDS_AT_END.get(t, ()):
                        add_out(g, m, left)
                    if t == BLOCKS:
                        last_y(BLOCKS - 2, 0, out_bank(BLOCKS - 2, left), slice(0, DM))
                    if t == BLOCKS + 1:
                        for k, cols in enumerate(halves):
                            last_y(BLOCKS - 1, k + 1, score_ps[:, k, 0:DM // 2], cols)

            moments_of(0)
            normalize_x(0)
            moments_of(1)
            turned_x_lo(0)
            split_first_w(1)
            normalize_x(1)
            split_first_w(2)
            split_first_w(3)
            turned_x_lo(1)
            dve.wait_ge(ffn_hi_done, 1)
            nc.vector.tensor_tensor(aw_lo[:, :, 0:LOW + EXPERTS], aw_raw[:, :, :], aw_hi[:, :, 0:LOW + EXPERTS].bitcast(F32),
                                    ALU.subtract).then_inc(ffn_lo_done, 1)
            moments_of(2)
            mean_square(0, 0)
            normalize_x(2)
            value_lo(0, 0)
            dve.wait_ge(small_loaded, 48)
            set_factor(0, 0)
            set_slope(0, 0)
            normalize_qk(0, 0)
            moments_of(3)
            router_logits(0)
            dve.wait_ge(ffn_hi_done, 2)
            nc.vector.tensor_tensor(bt_lo[:, :], bt_raw, bt_hi[:, :].bitcast(F32), ALU.subtract).then_inc(ffn_lo_done, 1)
            normalize_x(3)
            scale_low(0)
            turned_x_lo(2)
            moments_of(4)
            turned_x_lo(3)
            moments_of(5)
            mean_square(0, 1)
            turned_low_lo(0)
            normalize_x(4)
            normalize_x(5)
            value_lo(0, 1)
            turned_qk_lo(0, 0)
            normalize_qk(0, 1)
            bias(0, 0, 0)
            bias(0, 0, 1)
            router_logits(1)
            turned_x_lo(4)
            turned_x_lo(5)
            bias(0, 0, 2)
            bias(0, 0, 3)
            scale_low(1)
            moments_of(6)
            moments_of(7)
            turned_qk_lo(0, 1)
            turned_low_lo(1)
            normalize_x(6)
            normalize_x(7)
            normalize_probs(0, 0)
            mean_square(0, 2)
            value_lo(0, 2)
            turned_x_lo(6)
            normalize_qk(0, 2)
            turned_x_lo(7)
            router_logits(2)
            turned_lo(0, 0, 0)
            bias(0, 1, 0)
            bias(0, 1, 1)
            scale_low(2)
            router_logits(3)
            bias(0, 1, 2)
            bias(0, 1, 3)
            scale_low(3)
            turned_qk_lo(0, 2)
            turned_low_lo(2)
            normalize_probs(0, 1)
            mean_square(0, 3)
            value_lo(0, 3)
            turned_low_lo(3)
            mixed_lo(0, 0, GROUPS)
            normalize_qk(0, 3)
            for j in range(2):
                turned_lo(0, 1, j)
            dve.wait_ge(acc_ready, 1)
            pipeline(dve, slot)

        @block.tensor
        def _(pe):
            def three(out, a_hi, a_lo, b_hi, b_lo, start, stop):
                pe.matmul(out, a_hi, b_hi, start=start, stop=False)
                pe.matmul(out, a_hi, b_lo, start=False, stop=False)
                return pe.matmul(out, a_lo, b_hi, start=False, stop=stop)

            def project(g, t, chunks=range(KC)):
                m = t % BLOCKS
                rows = slice(m * P, (m + 1) * P)
                if 0 in chunks:
                    if t > 0:
                        pe.wait_ge(qk_norm_ready, ONE(g, t - 1, 1))
                        pe.wait_ge(v_lo_ready, ONE(g, t - 1, 1))
                    if t < 2:
                        pe.wait_ge(xt_lo_done, t + 1)
                for c in chunks:
                    if m == 0:
                        pe.wait_ge(w_lo_done, (g + t // BLOCKS) * KC + (c + 1))
                    for bank, lo, hi in ((0, 0, QW), (1, QW, QKV)):
                        last = three(qkv_ps[:, bank, 0:hi - lo], xt_hi[:, c, rows], xt_lo[:, c, rows],
                                     w_hi[:, c, lo:hi], w_lo[:, c, lo:hi], c == 0, c == KC - 1)
                if KC - 1 in chunks:
                    last.then_inc(qkv_ready, 1)

            def turn_x(t):
                pe.wait_ge(xn_done, t + 1)
                if t == 4:
                    pe.wait_ge(qk_hi_ready, 1)
                elif t == 5:
                    pe.wait_ge(qk_lo_ready, 1)
                elif t >= 6:
                    pe.wait_ge(qk_lo_ready, t - 4)
                elif t >= 2:
                    pe.wait_ge(xt_lo_done, t - 1)
                for c in range(KC):
                    tr = pe.transpose(turn_ps[:, t % 2, c * P:(c + 1) * P], x_sb[:, t, c * P:(c + 1) * P], ident)
                tr.then_inc(xt_turned, 1)

            def low_ranks(p):
                if p == 0:
                    pe.wait_ge(ffn_lo_done, 1)
                if p >= 2:
                    pe.wait_ge(gate_in_kept, p + 1)
                pe.wait_ge(xt_lo_done, 2 * p + 2)
                for b in range(2):
                    rows = slice((2 * p + b) * P, (2 * p + b + 1) * P)
                    for c in range(KC):
                        last = three(low_ps[p % 2][:, b, :], xt_hi[:, c, rows], xt_lo[:, c, rows],
                                     aw_hi[:, c, :], aw_lo[:, c, :], c == 0, c == KC - 1)
                last.then_inc(low_done, 1)

            def turn_low(p):
                pe.wait_ge(low_scaled, 2 * p + 2)
                if p == 1:
                    pe.wait_ge(biased_ready, PER_HEAD(0, 0, 3))
                elif p >= 2:
                    pe.wait_ge(biased_ready, PER_HEAD(0, 1, p + 1))
                for b in range(2):
                    tr = pe.transpose(lt_ps[p][:, b, :], low[:, p % 2, b, :], ident)
                tr.then_inc(low_turned, 1)

            def gate_in(t):
                if t == 0:
                    pe.wait_ge(ffn_lo_done, 2)
                pe.wait_ge(lt_lo_done, t // 2 + 1)
                if t in (2, 3):
                    pe.wait_ge(gate_in_kept, t - 1)
                elif t == 6:
                    pe.wait_ge(gate_in_kept, 6)
                elif t == 7:
                    pe.wait_ge(o_lo_ready, 1)
                a = t // 2 % 2
                three(gate_ps[t][:, :], lt_hi[:, a, t % 2, :], lt_lo[:, a, t % 2, :], bt_hi[:, :], bt_lo[:, :],
                      True, True).then_inc(gate_in_done, 1)

            def scores(g, t, h):
                n, hs, b = keys_of(t) * P, slice(h * HD, (h + 1) * HD), t // QB % BATCH
                if h == 0:
                    pe.wait_ge(qk_lo_ready, K_AND_Q_LO(g, t + 1, 0))
                    if t % QB == 0:
                        pe.wait_ge(k_full_ready, PER_BATCH(g, t, 1))
                if t > 0 or h >= 2:
                    pe.wait_ge(biased_ready, PER_HEAD(g, t, h - 1))
                if t < 2 and h == 0:
                    pe.wait_ge(lt_lo_done, t + 1)
                out = score_ps[:, h % 2, 0:n]
                if t % QB == 0:
                    last = pe.matmul(out, q_full[:, hs], k_full[:, :], start=True, stop=True)
                else:
                    last = three(out, q_hi[:, hs], q_lo[:, hs], k_hi[:, b, 0:n], k_lo[:, b, 0:n], True, True)
                last.then_inc(scores_ready, 1)

            def turn_q(g, u):
                t = u - 1
                pe.wait_ge(qk_norm_ready, ONE(g, u, 1))
                if u == 0:
                    pe.wait_ge(xt_lo_done, 4)
                elif u == 1:
                    pe.wait_ge(xt_lo_done, 6)
                elif u == 2:
                    pe.wait_ge(xt_lo_done, BLOCKS)
                elif (t - 1) % QB == 0:
                    pe.wait_ge(qk_lo_ready, K_AND_Q_LO(g, u, 0))
                    pe.wait_ge(pt_lo_ready, PER_KEY_BLOCK(g, t, 0))
                else:
                    pe.wait_ge(pt_lo_ready, PER_KEY_BLOCK(g, t, -1))
                for h in range(HPG):
                    tr = pe.transpose(turn_ps[:, turn_slot(t, 0), h * P:(h + 1) * P], qk_norm[:, h, :], ident)
                tr.then_inc(qk_turned, 1)

            def turn_k(g, u):
                t = u - 1
                if t > 0:
                    pe.wait_ge(pt_lo_ready, PER_KEY_BLOCK(g, t, 0))
                pe.transpose(turn_ps[:, turn_slot(t, 1), 0:P], qk_norm[:, HPG, :], ident).then_inc(qk_turned, 1)

            def turn_probs(g, t, j, left):
                if j >= 2:
                    pe.wait_ge(pt_lo_ready, PER_KEY_BLOCK(g, t, j - 1))
                elif t == 0:
                    pe.wait_ge(xt_lo_done, BLOCKS - 1)
                elif here(t + 1, left):
                    pe.wait_ge(qk_hi_ready, TWO(g, t + 1, j + 1))
                    if j == 1 or (t + 1) % QB > 0:
                        pe.wait_ge(qk_lo_ready, K_AND_Q_LO(g, t + 2, j - 1))
                else:
                    pe.wait_ge(pt_lo_ready, PER_KEY_BLOCK(g, t, 0))
                if j == 0:
                    pe.wait_ge(probs_ready, PER_HEAD(g, t, HPG))
                for h in range(HPG):
                    tr = pe.transpose(turn_ps[:, turn_slot(t, 2 + j), h * P:(h + 1) * P], probs[:, h, j * P:(j + 1) * P], ident)
                tr.then_inc(probs_turned, 1)

            def mix(g, u, j):
                i, b = u % QB, u // QB % BATCH
                pe.wait_ge(pt_lo_ready, PER_KEY_BLOCK(g, u, j + 1))
                if j == 0:
                    pe.wait_ge(v_lo_ready, ONE(g, u, 1))
                    if u > 0:
                        pe.wait_ge(o_lo_ready, ONE(g, u - 1, 1))
                    if u < 2:
                        pe.wait_ge(gate_in_kept, 5 + 3 * u)
                last = three(mix_ps[:, :], v_hi[:, b, j, :], v_lo[:, b, j, :], pt_hi[:, j, :], pt_lo[:, j, :], j == 0, j == i)
                if j == i:
                    last.then_inc(mix_ready, 1)

            def out(g, u, heads, left):
                hi, lo = o_parts(u, left)
                bank = out_bank(u, left)
                if 0 in heads:
                    pe.wait_ge(o_lo_ready, ONE(g, u, 1))
                    if u == 0:
                        pe.wait_ge(gate_in_kept, BLOCKS - 1)
                    elif left == 1 and u in (3, 4):
                        pe.wait_ge(qk_norm_ready, UNITS)
                        pe.wait_ge(v_lo_ready, UNITS)
                    elif left == 1 and u >= 5:
                        pe.wait_ge(acc_ready, 1 + ONE(g, u - 3, 1))
                    else:
                        pe.wait_ge(acc_ready, 1 + ONE(g, u - 1, 1))
                for h in heads:
                    if u % BLOCKS == 0:
                        pe.wait_ge(wo_lo_done, (g + u // BLOCKS) * HPG + (h + 1))
                    last = three(bank, hi[:, h, :], lo[:, h, :], wo_hi[:, h, :], wo_lo[:, h, :], h == 0, h == HPG - 1)
                if HPG - 1 in heads:
                    last.then_inc(out_ready, 1)

            def last_out(g, u):
                hi, lo = o_parts(u, 1)
                pe.wait_ge(o_lo_ready, ONE(g, u, 1))
                pe.wait_ge(biased_ready, PER_HEAD(g, u, HPG))
                for k, cols in enumerate(halves):
                    for h in range(HPG):
                        last = three(score_ps[:, k, 0:DM // 2], hi[:, h, :], lo[:, h, :],
                                     wo_hi[:, h, cols], wo_lo[:, h, cols], h == 0, h == HPG - 1)
                    last.then_inc(out_ready, 1)

            def slot(g, t, left):
                i, before = t % QB, (t - 1) % QB
                if here(t, left):
                    scores(g, t, 0)
                    if before == QB - 1:
                        scores(g, t, 1)
                if here(t - 1, left):
                    if before == QB - 1:
                        mix(g, t - 1, before - 1)
                        if here(t + 1, left):
                            turn_q(g, t + 1)
                    mix(g, t - 1, before)
                if here(t, left) and before < QB - 1:
                    scores(g, t, 1)
                if here(t + 1, left) and before < QB - 1:
                    turn_q(g, t + 1)
                if here(t, left):
                    scores(g, t, 2)
                if here(t + 1, left):
                    turn_k(g, t + 1)
                if here(t, left):
                    scores(g, t, 3)
                due = t - 1 if left > 1 else OUT_LATE.get(t)
                if here(t + 2, left):
                    project(g, t + 2, range(KC - 1 if held_back(t, left) else KC))
                if left == 1 and t in OUT_EARLY:
                    out(g, OUT_EARLY[t], range(HPG), left)
                if here(t, left):
                    turn_probs(g, t, 0, left)
                    if i >= 1:
                        turn_probs(g, t, 1, left)
                if due is not None:
                    out(g, due, range(0, 3), left)
                elif held_back(t, left):
                    project(g, t + 2, range(KC - 1, KC))
                elif t == BLOCKS - 1:
                    out(g, OUT_LAST, range(0, 2), left)
                if here(t, left) and i >= 2:
                    turn_probs(g, t, 2, left)
                if due is not None:
                    out(g, due, range(3, HPG), left)
                if here(t, left):
                    for j in range(min(i, 2)):
                        mix(g, t, j)
                        if j == 0 and i >= 3:
                            turn_probs(g, t, 3, left)
                if t == BLOCKS and left == 1:
                    out(g, OUT_LAST, range(2, HPG), left)
                    last_out(g, BLOCKS - 1)

            pe.wait_ge(aw_zeroed, 1)
            zeros = aw_hi[:, 0, :]
            for _ in range(WARMING):
                pe.matmul(score_ps[:, 0, 0:AW], zeros[:, 0:P], zeros, start=True, stop=True)
            pe.wait_ge(ident_loaded, 16)
            turn_x(0)
            project(0, 0, range(0, 2))
            turn_x(1)
            project(0, 0, range(2, KC))
            low_ranks(0)
            turn_x(2)
            project(0, 1, range(0, 2))
            turn_x(3)
            project(0, 1, range(2, KC))
            turn_low(0)
            turn_q(0, 0)
            turn_k(0, 0)
            low_ranks(1)
            turn_x(4)
            turn_x(5)
            scores(0, 0, 0)
            scores(0, 0, 1)
            gate_in(0)
            scores(0, 0, 2)
            scores(0, 0, 3)
            turn_q(0, 1)
            turn_k(0, 1)
            project(0, 2, range(0, 2))
            turn_low(1)
            project(0, 2, range(2, KC))
            gate_in(1)
            turn_x(6)
            turn_x(7)
            gate_in(2)
            gate_in(3)
            low_ranks(2)
            turn_probs(0, 0, 0, GROUPS)
            scores(0, 1, 0)
            scores(0, 1, 1)
            low_ranks(3)
            turn_q(0, 2)
            turn_k(0, 2)
            scores(0, 1, 2)
            scores(0, 1, 3)
            project(0, 3, range(0, 2))
            turn_low(2)
            project(0, 3, range(2, KC))
            gate_in(4)
            turn_low(3)
            gate_in(5)
            mix(0, 0, 0)
            turn_probs(0, 1, 0, GROUPS)
            turn_probs(0, 1, 1, GROUPS)
            gate_in(6)
            gate_in(7)
            out(0, 0, range(HPG), GROUPS)
            mix(0, 1, 0)
            pipeline(pe, slot)


def kernel(L0_attn_x, L0_attn_Wq, L0_attn_Wk, L0_attn_Wv, L0_attn_Wo, L0_attn_q_norm_w, L0_attn_k_norm_w,
           L0_ffn_A, L0_ffn_B, L0_ffn_Wr, L0_ffn_br):
    import concourse.bacc as bacc
    from concourse.bass_utils import run_bass_kernel_spmd

    def by_group(w, heads):
        return np.asarray(w).reshape(GROUPS, heads * HD, KC, P).transpose(0, 3, 2, 1)

    wqkv = np.concatenate([by_group(L0_attn_Wq, HPG), by_group(L0_attn_Wk, 1), by_group(L0_attn_Wv, 1)], axis=3)
    wo = np.asarray(L0_attn_Wo).reshape(DM, GROUPS, HPG, HD).transpose(1, 3, 2, 0)
    aw = np.concatenate([np.asarray(L0_ffn_A).reshape(LOW, DM), np.asarray(L0_ffn_Wr)], axis=0)
    aw = aw.reshape(LOW + EXPERTS, KC, P).transpose(2, 1, 0)
    arrays = {
        "x": np.asarray(L0_attn_x).reshape(BLOCKS * P, DM),
        "wqkv": wqkv.reshape(GROUPS, P, KC * QKV),
        "wo": wo.reshape(GROUPS, P, HPG * DM),
        "aw": aw.reshape(P, KC * (LOW + EXPERTS)),
        "bt": np.asarray(L0_ffn_B).transpose(0, 2, 1).reshape(LOW, DM),
        "br": np.broadcast_to(np.asarray(L0_ffn_br), (P, EXPERTS)),
        "qkw": np.stack([np.asarray(L0_attn_q_norm_w), np.asarray(L0_attn_k_norm_w)], axis=1),
        "consts": constants(),
    }
    arrays = {name: np.ascontiguousarray(a) for name, a in arrays.items()}
    nc = bacc.Bacc("TRN2", target_bir_lowering=False, num_devices=1)
    args = [nc.dram_tensor(name, a.shape, mybir.dt.from_np(a.dtype), kind="ExternalInput").ap() for name, a in arrays.items()]
    y = nc.dram_tensor("y", (BLOCKS * P, DM), F32, kind="ExternalOutput").ap()
    build(nc, *args, y)
    r = run_bass_kernel_spmd(nc, [arrays], core_ids=[0])
    return r.results[0]["y"].reshape(BATCH, SEQ, DM)
```
